# Optimizing a Trainium2 kernel written in Bass

```python
import numpy as np
import jax
import jax.numpy as jnp

def _softmax(x, axis=-1):
    return jax.nn.softmax(x, axis=axis)

def _gelu(x):
    return jax.nn.gelu(x, approximate=True)

def _silu(x):
    return jax.nn.silu(x)

def _sigmoid(x):
    return jax.nn.sigmoid(x)

def _layernorm(x, axis=-1, eps=1e-05):
    m = jnp.mean(x, axis=axis, keepdims=True)
    v = jnp.var(x, axis=axis, keepdims=True)
    return (x - m) / jnp.sqrt(v + eps)

def _scatter_add(tgt, idx, src, axis=0):
    return tgt.at[idx].add(src)

def _segment_sum(src, seg, n):
    return jax.ops.segment_sum(src, seg, n)
kernel_name = 'mk_sandwich_d1_jaxref_r4_43bb7a'

def setup_inputs(seed: int=0):
    np.random.seed(seed)
    _w = jnp.asarray

    def _L0_attn_setup():
        import jax, jax.numpy as jnp
        import numpy as np
        N_HEADS = 16
        EPS = 0.0001

        def _cosformer(x, Wq, bq, Wk, bk, Wv, bv, Wo, bo):
            B, L, E = x.shape
            H = N_HEADS
            hd = E // H
            q = jax.nn.relu(jnp.einsum('ble,fe->blf', x, Wq) + bq)
            k = jax.nn.relu(jnp.einsum('ble,fe->blf', x, Wk) + bk)
            v = jnp.einsum('ble,fe->blf', x, Wv) + bv

            def split_heads(t):
                return t.reshape(B, L, H, hd).transpose(0, 2, 1, 3).reshape(B * H, L, hd)
            q, k, v = (split_heads(q), split_heads(k), split_heads(v))
            m = L
            idx = np.pi / 2 * jnp.arange(1, m + 1, dtype=jnp.float32) / m
            sin = jnp.sin(idx)[None, :, None]
            cos = jnp.cos(idx)[None, :, None]
            q_ = jnp.concatenate([q * sin, q * cos], axis=-1)
            k_ = jnp.concatenate([k * sin, k * cos], axis=-1)
            kv = jnp.einsum('nld,nlm->ndm', k_, v)
            z = 1.0 / jnp.maximum(jnp.einsum('nld,nd->nl', q_, k_.sum(axis=1)), EPS)
            attn = jnp.einsum('nld,ndm->nlm', q_, kv) * z[:, :, None]
            out = attn.reshape(B, H, L, hd).transpose(0, 2, 1, 3).reshape(B, L, E)
            return jnp.einsum('ble,fe->blf', out, Wo) + bo
        key = jax.random.key(seed)
        ks = jax.random.split(key, 9)
        B, L, E = (4, 1024, 256)
        s = 1.0 / np.sqrt(E)
        return {'x': jax.random.normal(ks[0], (B, L, E), dtype=jnp.float32), 'Wq': jax.random.normal(ks[1], (E, E), dtype=jnp.float32) * s, 'bq': jax.random.normal(ks[2], (E,), dtype=jnp.float32) * 0.01, 'Wk': jax.random.normal(ks[3], (E, E), dtype=jnp.float32) * s, 'bk': jax.random.normal(ks[4], (E,), dtype=jnp.float32) * 0.01, 'Wv': jax.random.normal(ks[5], (E, E), dtype=jnp.float32) * s, 'bv': jax.random.normal(ks[6], (E,), dtype=jnp.float32) * 0.01, 'Wo': jax.random.normal(ks[7], (E, E), dtype=jnp.float32) * s, 'bo': jax.random.normal(ks[8], (E,), dtype=jnp.float32) * 0.01}
    _L0_attn_in = _L0_attn_setup()

    def _L0_ffn_setup():
        import jax, jax.numpy as jnp
        import numpy as np
        import math
        D_IN = 256
        FEATURES = (1024, 1024, 256)
        BATCH, SEQ = (8, 512)

        def _conn_dense(kernel_bool, x):
            w = jnp.where(kernel_bool, jnp.float32(1.0), jnp.float32(-1.0))
            return x @ w
        key = jax.random.key(seed)
        kx, kk0, kk1, kk2 = jax.random.split(key, 4)
        x = jax.random.normal(kx, (BATCH, SEQ, D_IN), dtype=jnp.float32)
        k0 = jax.random.randint(kk0, (2 * D_IN, FEATURES[0]), 0, 2).astype(jnp.bool_)
        k1 = jax.random.randint(kk1, (FEATURES[0], FEATURES[1]), 0, 2).astype(jnp.bool_)
        k2 = jax.random.randint(kk2, (FEATURES[1], FEATURES[2]), 0, 2).astype(jnp.bool_)
        s0 = jnp.asarray(1.0 / math.sqrt(2 * D_IN), dtype=jnp.float32)
        s1 = jnp.asarray(1.0 / math.sqrt(FEATURES[0]), dtype=jnp.float32)
        s2 = jnp.asarray(1.0 / math.sqrt(FEATURES[1]), dtype=jnp.float32)
        return {'x': x, 'k0': k0, 'k1': k1, 'k2': k2, 's0': s0, 's1': s1, 's2': s2}
    _L0_ffn_in = _L0_ffn_setup()
    _d = {'L0_attn_x': _L0_attn_in['x'], 'L0_attn_Wq': _L0_attn_in['Wq'], 'L0_attn_bq': _L0_attn_in['bq'], 'L0_attn_Wk': _L0_attn_in['Wk'], 'L0_attn_bk': _L0_attn_in['bk'], 'L0_attn_Wv': _L0_attn_in['Wv'], 'L0_attn_bv': _L0_attn_in['bv'], 'L0_attn_Wo': _L0_attn_in['Wo'], 'L0_attn_bo': _L0_attn_in['bo'], 'L0_ffn_k0': _L0_ffn_in['k0'], 'L0_ffn_k1': _L0_ffn_in['k1'], 'L0_ffn_k2': _L0_ffn_in['k2'], 'L0_ffn_s0': _L0_ffn_in['s0'], 'L0_ffn_s1': _L0_ffn_in['s1'], 'L0_ffn_s2': _L0_ffn_in['s2']}
    _x0 = _d['L0_attn_x']
    _d['L0_attn_x'] = jax.random.normal(jax.random.fold_in(jax.random.key(seed), 1), (2, 4096, 256), dtype=_x0.dtype)
    del _x0
    return _d

def reference(L0_attn_x, L0_attn_Wq, L0_attn_bq, L0_attn_Wk, L0_attn_bk, L0_attn_Wv, L0_attn_bv, L0_attn_Wo, L0_attn_bo, L0_ffn_k0, L0_ffn_k1, L0_ffn_k2, L0_ffn_s0, L0_ffn_s1, L0_ffn_s2):

    def _L0_attn_ref(x, Wq, bq, Wk, bk, Wv, bv, Wo, bo):
        import jax, jax.numpy as jnp
        import numpy as np
        N_HEADS = 16
        EPS = 0.0001

        def _cosformer(x, Wq, bq, Wk, bk, Wv, bv, Wo, bo):
            B, L, E = x.shape
            H = N_HEADS
            hd = E // H
            q = jax.nn.relu(jnp.einsum('ble,fe->blf', x, Wq) + bq)
            k = jax.nn.relu(jnp.einsum('ble,fe->blf', x, Wk) + bk)
            v = jnp.einsum('ble,fe->blf', x, Wv) + bv

            def split_heads(t):
                return t.reshape(B, L, H, hd).transpose(0, 2, 1, 3).reshape(B * H, L, hd)
            q, k, v = (split_heads(q), split_heads(k), split_heads(v))
            m = L
            idx = np.pi / 2 * jnp.arange(1, m + 1, dtype=jnp.float32) / m
            sin = jnp.sin(idx)[None, :, None]
            cos = jnp.cos(idx)[None, :, None]
            q_ = jnp.concatenate([q * sin, q * cos], axis=-1)
            k_ = jnp.concatenate([k * sin, k * cos], axis=-1)
            kv = jnp.einsum('nld,nlm->ndm', k_, v)
            z = 1.0 / jnp.maximum(jnp.einsum('nld,nd->nl', q_, k_.sum(axis=1)), EPS)
            attn = jnp.einsum('nld,ndm->nlm', q_, kv) * z[:, :, None]
            out = attn.reshape(B, H, L, hd).transpose(0, 2, 1, 3).reshape(B, L, E)
            return jnp.einsum('ble,fe->blf', out, Wo) + bo
        return _cosformer(x, Wq, bq, Wk, bk, Wv, bv, Wo, bo)

    def _L0_ffn_ref(x, k0, k1, k2, s0, s1, s2):
        import jax, jax.numpy as jnp
        import numpy as np
        import math
        D_IN = 256
        FEATURES = (1024, 1024, 256)
        BATCH, SEQ = (8, 512)

        def _conn_dense(kernel_bool, x):
            w = jnp.where(kernel_bool, jnp.float32(1.0), jnp.float32(-1.0))
            return x @ w
        h = jnp.concatenate([x, -x], axis=-1)
        h = s0 * _conn_dense(k0, h)
        h = jax.nn.relu(h) * 2
        h = s1 * _conn_dense(k1, h)
        h = jax.nn.relu(h) * 2
        h = s2 * _conn_dense(k2, h)
        return h
    x = L0_attn_x
    x = x + _layernorm(_L0_attn_ref(_layernorm(x, axis=-1), L0_attn_Wq, L0_attn_bq, L0_attn_Wk, L0_attn_bk, L0_attn_Wv, L0_attn_bv, L0_attn_Wo, L0_attn_bo), axis=-1)
    x = x + _layernorm(_L0_ffn_ref(_layernorm(x, axis=-1), L0_ffn_k0, L0_ffn_k1, L0_ffn_k2, L0_ffn_s0, L0_ffn_s1, L0_ffn_s2), axis=-1)
    return x

_drawn_inputs = setup_inputs


def setup_inputs(seed=0):
    import zlib

    import numpy as np

    out = dict(_drawn_inputs(seed))
    spreads = {}
    factors = {'L0_attn_bq': 7.55, 'L0_attn_bk': 8.0}
    for name, (base, spread) in spreads.items():
        noise = np.random.default_rng([zlib.crc32(name.encode()), seed]).standard_normal(out[name].shape)
        drawn = base * np.exp(spread * noise) if base else spread * noise
        out[name] = jnp.asarray(drawn.astype(out[name].dtype))
    for name, factor in factors.items():
        out[name] = (out[name] * factor).astype(out[name].dtype)
    return out
```

```python
from contextlib import ExitStack

import numpy as np

import concourse.bass as bass
from concourse import mybir

F32 = mybir.dt.float32
F32R = mybir.dt.float32r
F16 = mybir.dt.float16
U8 = mybir.dt.uint8
U32 = mybir.dt.uint32
ALU = mybir.AluOpType
ACT = mybir.ActivationFunctionType

P = 128
B, L, E = 2, 4096, 256
HEADS = 16
HD = E // HEADS
F = 1024
T = 4
CH = T * P
NB = L // CH
NCH = B * NB
KE = E // P
KF = F // P
G = 4
GW = E // G
VW = P + 1
EPS_DEN = 1e-4
EPS_LN = 1e-5
H1_SCALE = 2.0 ** -4
OUT_SCALE = 8.0 / H1_SCALE


def shape_tables():
    idx = (np.float32(np.pi / 2) * np.arange(1, L + 1, dtype=np.float32) / np.float32(L)).astype(np.float32)
    sc = np.stack([np.sin(idx), np.cos(idx)]).astype(np.float32)
    by = sc.reshape(2, NB, P, T)
    rows = np.ascontiguousarray(by.transpose(1, 0, 3, 2)).reshape(NB, 2 * CH)
    cols = np.ascontiguousarray(by.transpose(2, 1, 3, 0)).reshape(P, NB * T * 2)
    ident = np.eye(P, dtype=np.float32)
    r, c = np.arange(P)[:, None] % GW, np.arange(GW)[None, :]
    mask = (r // HD == c // HD).astype(np.float32)
    return rows, cols, ident, mask


def build(nc, x, wq_t, wkv_t, wo_t, bq, bkv, bo, k0, k1, k2, scales, rows_d, cols_d, ident_d, mask_d, out):
    ctx = ExitStack()
    with ctx:
        def sb(name, shape, dt=F32):
            return ctx.enter_context(nc.sbuf_tensor(name, shape, dt))

        def sem(name):
            return ctx.enter_context(nc.semaphore(name))

        ident = sb("ident", [P, P])
        mask = sb("mask", [P, GW])
        pos_cols = sb("pos_cols", [P, NB, T, 2])
        pos_hi = sb("pos_hi", [P, NB, T, 2], F32R)
        pos_lo = sb("pos_lo", [P, NB, T, 2], F32R)
        wq_hi = sb("wq_hi", [P, KE, E], F32R)
        wq_lo = sb("wq_lo", [P, KE, E], F32R)
        wkv_hi = sb("wkv_hi", [P, KE, 2 * E], F32R)
        wkv_lo = sb("wkv_lo", [P, KE, 2 * E], F32R)
        wo_hi = sb("wo_hi", [P, KE, E], F32R)
        wo_lo = sb("wo_lo", [P, KE, E], F32R)
        bq_col = sb("bq_col", [P, KE])
        bkv_row = sb("bkv_row", [P, 2 * E])
        bo_row = sb("bo_row", [P, E])
        w0 = sb("w0", [P, KE, F], F16)
        w1 = sb("w1", [P, KF, F], F16)
        w2 = sb("w2", [P, KF, E], F16)
        sv = sb("sv", [P, 3])
        sgn = sb("sgn", [P, 3])
        sab = sb("sab", [P, 3])
        ksc = sb("ksc", [P, 4])
        ocs = sb("ocs", [P, 3])

        xa = sb("xa", [P, T, E])
        xn = sb("xn", [P, T, E])
        xt_hi = sb("xt_hi", [P, KE, CH], F32R)
        xt_lo = sb("xt_lo", [P, KE, CH], F32R)
        q_all = sb("q_all", [P, KE, L])
        kv = sb("kv", [P, 2, 2 * E])
        k_hi = sb("k_hi", [P, 2, E], F32R)
        k_lo = sb("k_lo", [P, 2, E], F32R)
        v_hi = sb("v_hi", [P, 2, KE, 2, VW], F32R)
        v_lo = sb("v_lo", [P, 2, KE, 2, VW], F32R)
        eps_col = sb("eps_col", [P, 1])
        zero_l = sb("zero_l", [P, P], F32R)
        kvt_hi = sb("kvt_hi", [P, G, P], F32R)
        kvt_lo = sb("kvt_lo", [P, G, P], F32R)

        pos_rows = sb("pos_rows", [P, 2, CH])
        qsc = sb("qsc", [P, G, CH])
        qsc_hi = sb("qsc_hi", [P, G, CH], F32R)
        qsc_lo = sb("qsc_lo", [P, G, CH], F32R)
        att = sb("att", [P, KE, CH])
        att_hi = sb("att_hi", [P, KE, CH], F32R)
        att_lo = sb("att_lo", [P, KE, CH], F32R)
        x1n = sb("x1n", [P, T, E])
        ob = sb("ob", [P, T, E])
        x1 = sb("x1", [P, T, E])
        kv_sum = ob[:].rearrange("p t e -> p (t e)")[:, 0:KE * 2 * VW].rearrange("p (h s c) -> p h s c", h=KE, s=2)
        kvt = att[:, 0, :].rearrange("p (g m) -> p g m", g=G)
        x2_hi = sb("x2_hi", [P, KE, CH], F16)
        x2_lo = sb("x2_lo", [P, KE, CH], F16)
        h1_hi = sb("h1_hi", [P, KF, CH], F16)
        h1_lo = sb("h1_lo", [P, KF, CH], F16)
        h2_hi = sb("h2_hi", [P, KF, CH], F16)
        h2_lo = sb("h2_lo", [P, KF, CH], F16)
        fo = sb("fo", [P, T, E])

        wq_f = qsc[:, 0, :].rearrange("p (k e) -> p k e", k=KE)
        wo_f = qsc[:, 1, :].rearrange("p (k e) -> p k e", k=KE)
        wkv_f = qsc[:, 2:4, :]
        k1_u8 = h1_hi[:].bitcast(U8).rearrange("p k c -> p (k c)").rearrange("p (k f) -> p k f", k=KF)
        k0_u8 = h1_lo[:].bitcast(U8).rearrange("p k c -> p (k c)")[:, 0:4 * F].rearrange("p (k f) -> p k f", k=4)
        k2_u8 = h1_lo[:].bitcast(U8).rearrange("p k c -> p (k c)")[:, 4 * F:4 * F + KF * E].rearrange(
            "p (k f) -> p k f", k=KF)
        w0_half = h2_hi[:].rearrange("p k c -> p (k c)").rearrange("p (k f) -> p k f", k=4)

        class Norm:

            def __init__(self, name):
                self.stats = sb(name + "_stats", [P, T, 6])
                self.d = sb(name + "_d", [P, 4, T])
                self.mean = sb(name + "_mean", [P, T])
                self.var = sb(name + "_var", [P, T])
                self.std = sb(name + "_std", [P, T])
                self.rstd = sb(name + "_rstd", [P, T])
                self.nmr = sb(name + "_nmr", [P, T])
                self.s_stats = sem(name + "_stats_done")
                self.s_d = sem(name + "_d_done")
                self.s_d2 = sem(name + "_d2_done")
                self.s_mean = sem(name + "_mean_done")
                self.s_var = sem(name + "_var_done")
                self.s_std = sem(name + "_std_done")
                self.s_rstd = sem(name + "_rstd_done")
                self.s_nmr = sem(name + "_nmr_done")

        ln_a, ln_o, ln_2, ln_f = Norm("ln_a"), Norm("ln_o"), Norm("ln_2"), Norm("ln_f")

        def bank(name):
            return ctx.enter_context(nc.psum_tensor(name, [P, 512], F32))

        acc = [bank("acc0"), bank("acc1")]
        ffp = [bank("ffp0"), bank("ffp1")]
        yp = [bank("yp0"), bank("yp1")]
        wp = [bank("wp0"), bank("wp1")]

        s_first = sem("first_loads")
        s_late = sem("late_loads")
        s_xa = sem("xa_loaded")
        s_xr = sem("xr_loaded")
        s_rows = sem("pos_rows_loaded")
        s_free = sem("fo_free")
        s_whi = sem("w_hi_ready")
        s_wlo = sem("w_lo_ready")
        s_zero = sem("zero_ready")
        s_poshi = sem("pos_hi_ready")
        s_poslo = sem("pos_lo_ready")
        s_sc = sem("scale_terms")
        s_w0h = sem("w0_halves")
        s_ffw = sem("ffn_weights_ready")

        s_xn = sem("xn_ready")
        s_xtp = sem("xt_in_psum")
        s_xth = sem("xt_hi_ready")
        s_xtl = sem("xt_lo_ready")
        s_qp = sem("q_in_psum")
        s_q = sem("q_kept")
        s_kvp = sem("kv_in_psum")
        s_kv = sem("kv_biased")
        s_hi = sem("kv_hi_ready")
        s_lo = sem("kv_lo_ready")
        s_pc = sem("pos_in_v")
        s_acc = sem("acc_step_done")
        s_accz = sem("acc_closed")
        s_sum = sem("kv_sum_ready")
        s_kvz = sem("kvt_cleared")
        s_kvt = sem("kvt_ready")
        s_kvh = sem("kvt_hi_ready")
        s_kvl = sem("kvt_lo_ready")

        s_qs = sem("q_sin_ready")
        s_qc = sem("q_cos_ready")
        s_qh = sem("qsc_hi_ready")
        s_ql = sem("qsc_lo_ready")
        s_atp = sem("att_in_psum")
        s_den = sem("den_ready")
        s_rden = sem("rden_ready")
        s_att = sem("att_ready")
        s_ath = sem("att_hi_ready")
        s_atl = sem("att_lo_ready")
        s_op = sem("o_in_psum")
        s_ob = sem("o_biased")
        s_on = sem("o_normed")
        s_x1n = sem("x1n_ready")
        s_x1 = sem("x1_kept")
        s_xn2 = sem("xn2_ready")
        s_x2p = sem("x2_in_psum")
        s_x2h = sem("x2_hi_ready")
        s_x2l = sem("x2_lo_ready")

        s_hp = sem("h_in_psum")
        s_hh = sem("h_hi_ready")
        s_hl = sem("h_lo_ready")
        s_yp = sem("y_in_psum")
        s_fc = sem("f_scale_ready")
        s_fo = sem("f_normed")
        s_out = sem("out_ready")

        x_c = x.rearrange("(c p t) e -> c p (t e)", p=P, t=T)
        out_c = out.rearrange("(c p t) e -> c p (t e)", p=P, t=T)

        def pick(ap, i):
            return ap[bass.ds(i, 1)].rearrange("o p f -> (o p) f")

        FIRST_LOADS, LATE_LOADS = 8, 9
        block = ctx.enter_context(nc.Block())

        @block.sync
        def _(sp):
            def load_x(a):
                src = pick(x_c, a)
                sp.wait_ge(s_xn, a * T)
                sp.dma_start(xa[:].rearrange("p t e -> p (t e)"), src).then_inc(s_xa, 16)

            def load_rows(c, pos):
                src = rows_d[bass.ds(pos, 1), :].to_broadcast([P, 2 * CH])
                sp.wait_ge(s_qs, c * G)
                sp.wait_ge(s_qc, c * G)
                sp.dma_start(pos_rows[:].rearrange("p s c -> p (s c)"), src).then_inc(s_rows, 16)

            def load_xr(c):
                src = pick(x_c, c)
                sp.wait_ge(s_x1, c)
                sp.wait_ge(s_xn2, c * T)
                sp.dma_start(x1n[:].rearrange("p t e -> p (t e)"), src).then_inc(s_xr, 16)

            def store(f):
                dst = pick(out_c, f)
                sp.wait_ge(s_out, f + 1)
                sp.dma_start(dst, fo[:].rearrange("p t e -> p (t e)")).then_inc(s_free, 16)

            sp.dma_start(xa[:].rearrange("p t e -> p (t e)"), x_c[0]).then_inc(s_xa, 16)
            sp.dma_start(ident[:], ident_d).then_inc(s_first, 16)
            sp.dma_start(wkv_f, wkv_t.rearrange("(k p) f -> p k f", p=P)).then_inc(s_first, 16)
            sp.dma_start(wq_f, wq_t.rearrange("(k p) f -> p k f", p=P)).then_inc(s_first, 16)
            sp.dma_start(wo_f, wo_t.rearrange("(k p) f -> p k f", p=P)).then_inc(s_first, 16)
            sp.dma_start(bq_col[:], bq.rearrange("(k p) -> p k", p=P), allow_slow_non_contiguous=True).then_inc(s_first, 16)
            sp.dma_start(bkv_row[:], bkv.to_broadcast([P, 2 * E])).then_inc(s_first, 16)
            sp.dma_start(bo_row[:], bo.to_broadcast([P, E])).then_inc(s_first, 16)
            sp.dma_start(pos_cols[:].rearrange("p c t s -> p (c t s)"), cols_d).then_inc(s_first, 16)
            sp.dma_start(mask[:], mask_d).then_inc(s_late, 16)
            for n in range(3):
                sp.dma_start(sv[:, n:n + 1], scales[n].to_broadcast([P, 1]),
                             allow_slow_non_contiguous=True).then_inc(s_late, 16)
            sp.dma_start(k0_u8.bitcast(U32), k0.rearrange("(k p) f -> p k f", p=P)).then_inc(s_late, 16)
            half = KF // 2
            sp.dma_start(k1_u8[:, 0:half].bitcast(U32), k1[0:half * P].rearrange("(k p) f -> p k f", p=P)).then_inc(s_late, 16)
            sp.dma_start(k1_u8[:, half:KF].bitcast(U32), k1[half * P:F].rearrange("(k p) f -> p k f", p=P)).then_inc(s_late, 16)
            sp.dma_start(k2_u8[:, 0:half].bitcast(U32), k2[0:half * P].rearrange("(k p) f -> p k f", p=P)).then_inc(s_late, 16)
            sp.dma_start(k2_u8[:, half:KF].bitcast(U32), k2[half * P:F].rearrange("(k p) f -> p k f", p=P)).then_inc(s_late, 16)
            load_rows(0, 0)
            load_xr(0)
            with sp.Fori(1, NB + 1) as a:
                load_x(a)
            with sp.Fori(0, NB - 1) as f:
                load_rows(f + 1, f + 1)
                load_xr(f + 1)
                load_x(f + (NB + 1))
                store(f)
            load_rows(NB, 0)
            load_xr(NB)
            store(NB - 1)
            with sp.Fori(NB, NCH - 1) as f:
                load_rows(f + 1, f - (NB - 1))
                load_xr(f + 1)
                store(f)
            store(NCH - 1)
            sp.wait_ge(s_free, 16 * (NCH + 1))

        @block.tensor
        def _(pe):
            def mm(dst, lhs, rhs, start, stop):
                return nc.tensor.matmul(dst, lhs, rhs, start=start, stop=stop)

            def passes(dst, pairs, acc_open=False):
                last = None
                n = 0
                for (lh, ll), (rh, rl) in pairs:
                    for u, v in ((lh, rh), (lh, rl), (ll, rh)):
                        last = mm(dst, u, v, n == 0 and not acc_open, n == 3 * len(pairs) - 1 and not acc_open)
                        n += 1
                return last

            def transpose_x(a):
                pe.wait_ge(s_xn, a * T + T)
                for h in range(KE):
                    for t in range(T):
                        last = nc.tensor.transpose(wp[h][:, t * P:(t + 1) * P], xn[:, t, h * P:(h + 1) * P], ident[:])
                    last.then_inc(s_xtp, 1)

            def project_q(a):
                pe.wait_ge(s_xtl, a * KE + KE)
                for h in range(KE):
                    m = slice(h * P, (h + 1) * P)
                    passes(wp[h][:], [((wq_hi[:, k, m], wq_lo[:, k, m]), (xt_hi[:, k, :], xt_lo[:, k, :]))
                                      for k in range(KE)]).then_inc(s_qp, 1)

            def project_kv(a, t):
                if t < 2:
                    pe.wait_ge(s_q, a * KE + t + 1)
                else:
                    pe.wait_ge(s_kv, a * T + t - 1)
                m = slice(t * P, (t + 1) * P)
                passes(wp[t % 2][:], [((xt_hi[:, k, m], xt_lo[:, k, m]), (wkv_hi[:, k, :], wkv_lo[:, k, :]))
                                      for k in range(KE)]).then_inc(s_kvp, 1)

            def sum_kv(a, t):
                pe.wait_ge(s_lo, (a * T + t + 1) * 3)
                pe.wait_ge(s_pc, (a * T + t + 1) * 2)
                b = t % 2
                for h in range(KE):
                    m = slice(h * P, (h + 1) * P)
                    last = passes(acc[h][:, 0:2 * VW], [((k_hi[:, b, m], k_lo[:, b, m]),
                                  (v_hi[:, b, h].rearrange("p s c -> p (s c)"),
                                   v_lo[:, b, h].rearrange("p s c -> p (s c)")))], acc_open=True)
                last.then_inc(s_acc, 1)

            def open_acc():
                for h in range(KE):
                    mm(acc[h][:, 0:2 * VW], zero_l[:], wkv_hi[:, 0, 0:2 * VW], True, False)

            def close_acc():
                for h in range(KE):
                    last = mm(acc[h][:, 0:2 * VW], zero_l[:], wkv_hi[:, 0, 0:2 * VW], False, True)
                last.then_inc(s_accz, 1)

            def attend(c, g):
                pe.wait_ge(s_ql, c * G + g + 1)
                if g >= 2:
                    pe.wait_ge(s_att, c * G + g - 1)
                passes(wp[g % 2][:], [((kvt_hi[:, g, :], kvt_lo[:, g, :]), (qsc_hi[:, g, :], qsc_lo[:, g, :]))]
                       ).then_inc(s_atp, 1)

            def project_o(c):
                pe.wait_ge(s_atl, c * KE + KE)
                for t in range(T):
                    m = slice(t * P, (t + 1) * P)
                    last = passes(wp[t // 2][:, (t % 2) * E:(t % 2 + 1) * E],
                                  [((att_hi[:, k, m], att_lo[:, k, m]), (wo_hi[:, k, :], wo_lo[:, k, :]))
                                   for k in range(KE)])
                    if t % 2:
                        last.then_inc(s_op, 1)

            def transpose_x2(c):
                pe.wait_ge(s_xn2, c * T + T)
                for h in range(KE):
                    for t in range(T):
                        last = nc.tensor.transpose(wp[h][:, t * P:(t + 1) * P], ob[:, t, h * P:(h + 1) * P], ident[:])
                    last.then_inc(s_x2p, 1)

            def hidden(f, n, w, hi, lo, kn):
                j = n % KF
                if n >= 2:
                    pe.wait_ge(s_hl, f * 2 * KF + n - 1)
                m = slice(j * P, (j + 1) * P)
                for k in range(kn):
                    mm(ffp[n % 2][:], w[:, k, m], hi[:, k, :], k == 0, False)
                    last = mm(ffp[n % 2][:], w[:, k, m], lo[:, k, :], False, k == kn - 1)
                last.then_inc(s_hp, 1)

            def layer0(f):
                pe.wait_ge(s_x2l, f * KE + KE)
                for j in range(KF):
                    hidden(f, j, w0, x2_hi, x2_lo, KE)

            def layer1(f, j):
                if j == 0:
                    pe.wait_ge(s_hl, f * 2 * KF + KF)
                hidden(f, KF + j, w1, h1_hi, h1_lo, KF)

            def layer2(f, t):
                if t == 0:
                    pe.wait_ge(s_hl, (f + 1) * 2 * KF)
                m = slice(t * P, (t + 1) * P)
                dst = yp[t // 2][:, (t % 2) * E:(t % 2 + 1) * E]
                for k in range(KF):
                    mm(dst, h2_hi[:, k, m], w2[:, k, :], k == 0, False)
                    last = mm(dst, h2_lo[:, k, m], w2[:, k, :], False, k == KF - 1)
                last.then_inc(s_yp, 1)

            pe.wait_ge(s_first, 16 * FIRST_LOADS)
            transpose_x(0)
            pe.wait_ge(s_wlo, 3)
            pe.wait_ge(s_zero, 1)
            open_acc()
            with pe.Fori(0, NB) as a:
                project_q(a)
                project_kv(a, 0)
                project_kv(a, 1)
                sum_kv(a, 0)
                project_kv(a, 2)
                sum_kv(a, 1)
                project_kv(a, 3)
                pe.wait_ge(s_kv, a * T + T)
                transpose_x(a + 1)
                sum_kv(a, 2)
                sum_kv(a, 3)
            close_acc()
            pe.wait_ge(s_sum, KE)
            open_acc()
            pe.wait_ge(s_xtl, NB * KE + KE)
            pe.wait_ge(s_kvl, 1)
            for g in range(G):
                attend(0, g)
            project_o(0)
            transpose_x2(0)
            pe.wait_ge(s_ffw, 3)
            with pe.Fori(0, NB - 1) as f:
                c, a = f + 1, f + NB
                layer0(f)
                pe.wait_ge(s_x2l, f * KE + KE)
                attend(c, 0)
                attend(c, 1)
                layer1(f, 0)
                attend(c, 2)
                attend(c, 3)
                layer1(f, 1)
                project_o(c)
                layer1(f, 2)
                pe.wait_ge(s_ob, c * 2 + 2)
                project_q(a)
                layer1(f, 3)
                project_kv(a, 0)
                project_kv(a, 1)
                layer1(f, 4)
                sum_kv(a, 0)
                project_kv(a, 2)
                layer1(f, 5)
                sum_kv(a, 1)
                project_kv(a, 3)
                layer1(f, 6)
                sum_kv(a, 2)
                pe.wait_ge(s_kv, a * T + T)
                transpose_x2(c)
                layer1(f, 7)
                sum_kv(a, 3)
                layer2(f, 0)
                pe.wait_ge(s_x2l, c * KE + KE)
                transpose_x(a + 1)
                layer2(f, 1)
                layer2(f, 2)
                layer2(f, 3)
            f = NB - 1
            c, a = NB, NCH - 1
            layer0(f)
            project_q(a)
            project_kv(a, 0)
            project_kv(a, 1)
            layer1(f, 0)
            sum_kv(a, 0)
            project_kv(a, 2)
            layer1(f, 1)
            sum_kv(a, 1)
            project_kv(a, 3)
            layer1(f, 2)
            sum_kv(a, 2)
            sum_kv(a, 3)
            close_acc()
            for j in range(3, KF):
                layer1(f, j)
                if j == 4:
                    pe.wait_ge(s_kvl, 2)
                    pe.wait_ge(s_kv, NCH * T)
                    attend(c, 0)
                    attend(c, 1)
                if j == 5:
                    attend(c, 2)
                    attend(c, 3)
                if j == 7:
                    project_o(c)
            for t in range(T):
                layer2(f, t)
            transpose_x2(c)
            with pe.Fori(NB, NCH - 1) as f:
                c = f + 1
                layer0(f)
                attend(c, 0)
                attend(c, 1)
                layer1(f, 0)
                attend(c, 2)
                attend(c, 3)
                layer1(f, 1)
                project_o(c)
                for j in range(2, 7):
                    layer1(f, j)
                transpose_x2(c)
                layer1(f, 7)
                for t in range(T):
                    layer2(f, t)
            f = NCH - 1
            layer0(f)
            for j in range(KF):
                layer1(f, j)
            for t in range(T):
                layer2(f, t)

        @block.scalar
        def _(act):
            def std(ln, n, scale=1.0 / E):
                act.wait_ge(ln.s_var, n + 1)
                nc.scalar.activation(ln.std[:], ln.var[:], ACT.Sqrt, bias=eps_col[:], scale=scale
                                     ).then_inc(ln.s_std, 1)

            def split_x(a):
                for h in range(KE):
                    act.wait_ge(s_xtp, a * KE + h + 1)
                    nc.scalar.activation(xt_hi[:, h, :], wp[h][:], ACT.Copy).then_inc(s_xth, 1)

            def keep_q(a, pos):
                for h in range(KE):
                    act.wait_ge(s_qp, a * KE + h + 1)
                    nc.scalar.activation(q_all[:, h, bass.ds(pos * CH, CH)], wp[h][:], ACT.Relu,
                                         bias=bq_col[:, h:h + 1]).then_inc(s_q, 1)

            def split_kv(a, t, pos):
                b = t % 2
                act.wait_ge(s_kv, a * T + t + 1)
                if t >= 2:
                    act.wait_ge(s_acc, a * T + t - 1)
                nc.scalar.activation(k_hi[:, b, :], kv[:, b, 0:E], ACT.Relu).then_inc(s_hi, 1)
                v = kv[:, b, E:2 * E].rearrange("p (h c) -> p h c", h=KE)
                for s in range(2):
                    at = pos_cols[:, bass.ds(pos, 1), t, s:s + 1].rearrange("p o s -> p (o s)")
                    nc.scalar.activation(v_hi[:, b, :, s, 0:P], v, ACT.Copy, scale=at).then_inc(s_hi, 1)

            def split_q(c):
                for g in range(G):
                    act.wait_ge(s_qs, c * G + g + 1)
                    act.wait_ge(s_qc, c * G + g + 1)
                    if g == 0:
                        act.wait_ge(s_atp, c * G)
                    nc.scalar.activation(qsc_hi[:, g, :], qsc[:, g, :], ACT.Copy).then_inc(s_qh, 1)

            def split_att(c, k):
                act.wait_ge(s_att, c * G + 2 * k + 2)
                act.wait_ge(s_op, c * 2)
                nc.scalar.activation(att_hi[:, k, :], att[:, k, :], ACT.Copy).then_inc(s_ath, 1)

            def split_x2(c):
                for h in range(KE):
                    act.wait_ge(s_x2p, c * KE + h + 1)
                    nc.scalar.activation(x2_hi[:, h, :], wp[h][:], ACT.Copy).then_inc(s_x2h, 1)

            def hidden(f, n):
                act.wait_ge(s_hp, f * 2 * KF + n + 1)
                dst = (h1_hi if n < KF else h2_hi)[:, n % KF, :]
                nc.scalar.activation(dst, ffp[n % 2][:], ACT.Relu).then_inc(s_hh, 1)

            def layer0(f):
                for n in range(KF):
                    hidden(f, n)

            def keep_x1(f):
                act.wait_ge(s_x1n, f + 1)
                if isinstance(f, int) and f == NCH - 1:
                    act.wait_ge(s_out, f)
                nc.scalar.copy(x1[:], x1n[:]).then_inc(s_x1, 1)

            def norm_y(f):
                act.wait_ge(ln_f.s_nmr, f + 1)
                act.wait_ge(s_free, f * 16 + 16)
                for t in range(T):
                    nc.scalar.activation(fo[:, t, :], yp[t // 2][:, (t % 2) * E:(t % 2 + 1) * E], ACT.Identity,
                                         bias=ln_f.nmr[:, t:t + 1], scale=ln_f.std[:, t:t + 1]).then_inc(s_fo, 1)

            act.sem_inc(s_free, 16)
            act.wait_ge(s_zero, 2)
            act.wait_ge(s_first, 16 * FIRST_LOADS)
            std(ln_a, 0)
            nc.scalar.activation(wkv_hi[:], wkv_f, ACT.Copy).then_inc(s_whi, 1)
            nc.scalar.activation(wq_hi[:], wq_f, ACT.Copy).then_inc(s_whi, 1)
            split_x(0)
            nc.scalar.activation(wo_hi[:], wo_f, ACT.Copy).then_inc(s_whi, 1)
            with act.Fori(0, NB) as a:
                keep_q(a, a)
                split_kv(a, 0, a)
                split_kv(a, 1, a)
                std(ln_a, a + 1)
                split_kv(a, 2, a)
                split_kv(a, 3, a)
                split_x(a + 1)
            split_q(0)
            split_att(0, 0)
            split_att(0, 1)
            std(ln_o, 0)
            std(ln_2, 0)
            split_x2(0)
            with act.Fori(0, NB - 1) as f:
                c, a, pos = f + 1, f + NB, f
                layer0(f)
                split_q(c)
                keep_x1(f)
                hidden(f, 8)
                split_att(c, 0)
                hidden(f, 9)
                split_att(c, 1)
                hidden(f, 10)
                std(ln_o, c)
                keep_q(a, pos)
                hidden(f, 11)
                split_kv(a, 0, pos)
                hidden(f, 12)
                split_kv(a, 1, pos)
                std(ln_2, c)
                std(ln_a, a + 1)
                hidden(f, 13)
                split_kv(a, 2, pos)
                hidden(f, 14)
                split_kv(a, 3, pos)
                split_x2(c)
                hidden(f, 15)
                split_x(a + 1)
                std(ln_f, f, ocs[:, 2:3])
                norm_y(f)
            f = NB - 1
            c, a, pos = NB, NCH - 1, NB - 1
            layer0(f)
            keep_q(a, pos)
            split_kv(a, 0, pos)
            hidden(f, 8)
            split_kv(a, 1, pos)
            hidden(f, 9)
            split_kv(a, 2, pos)
            split_kv(a, 3, pos)
            hidden(f, 10)
            hidden(f, 11)
            split_q(c)
            keep_x1(f)
            hidden(f, 12)
            split_att(c, 0)
            hidden(f, 13)
            split_att(c, 1)
            hidden(f, 14)
            hidden(f, 15)
            std(ln_o, c)
            std(ln_2, c)
            std(ln_f, f, ocs[:, 2:3])
            norm_y(f)
            split_x2(c)
            with act.Fori(NB, NCH - 1) as f:
                c = f + 1
                layer0(f)
                split_q(c)
                keep_x1(f)
                hidden(f, 8)
                split_att(c, 0)
                hidden(f, 9)
                split_att(c, 1)
                hidden(f, 10)
                std(ln_o, c)
                hidden(f, 11)
                hidden(f, 12)
                std(ln_2, c)
                hidden(f, 13)
                hidden(f, 14)
                split_x2(c)
                hidden(f, 15)
                std(ln_f, f, ocs[:, 2:3])
                norm_y(f)
            f = NCH - 1
            keep_x1(f)
            for n in range(2 * KF):
                hidden(f, n)
            std(ln_f, f, ocs[:, 2:3])
            norm_y(f)

        @block.vector
        def _(dve):
            def low(dst, src, hi, sign_op=None, scalar=0.0):
                return nc.vector.scalar_tensor_tensor(out=dst, in0=src, scalar=scalar, in1=hi,
                                                      op0=sign_op, op1=ALU.subtract)

            def stats(ln, n, tiles, free=None):
                for t in range(T):
                    if free is not None:
                        free(t)
                    nc.vector.bn_stats(ln.stats[:, t, :], tiles[t]).then_inc(ln.s_stats, 1)
                dve.wait_ge(ln.s_stats, n * T + T)
                even, odd = ln.stats[:, :, 1], ln.stats[:, :, 4]
                nc.vector.tensor_tensor(ln.d[:, 1, :], even, odd, ALU.subtract).then_inc(ln.s_d, 1)
                nc.vector.tensor_tensor(ln.d[:, 0, :], even, odd, ALU.add).then_inc(ln.s_d, 1)
                nc.vector.tensor_tensor(ln.d[:, 2, :], ln.stats[:, :, 2], ln.stats[:, :, 5], ALU.add
                                        ).then_inc(ln.s_d, 1)
                dve.wait_ge(ln.s_d, n * 3 + 3)
                nc.vector.tensor_tensor(ln.d[:, 3, :], ln.d[:, 1, :], ln.d[:, 1, :], ALU.mult).then_inc(ln.s_d2, 1)
                nc.vector.tensor_scalar(ln.mean[:], ln.d[:, 0, :], 0.5, None, ALU.mult).then_inc(ln.s_mean, 1)
                dve.wait_ge(ln.s_d2, n + 1)
                nc.vector.scalar_tensor_tensor(out=ln.var[:], in0=ln.d[:, 3, :], scalar=E / 4.0, in1=ln.d[:, 2, :],
                                               op0=ALU.mult, op1=ALU.add).then_inc(ln.s_var, 1)

            def rstd(ln, n):
                dve.wait_ge(ln.s_std, n + 1)
                nc.vector.reciprocal(ln.rstd[:], ln.std[:]).then_inc(ln.s_rstd, 1)
                dve.wait_ge(ln.s_rstd, n + 1)
                dve.wait_ge(ln.s_mean, n + 1)

            def norm_tiles(ln, dst, src, done):
                for t in range(T):
                    nc.vector.tensor_scalar(dst[:, t, :], src[:, t, :], ln.mean[:, t:t + 1], ln.rstd[:, t:t + 1],
                                            ALU.subtract, ALU.mult).then_inc(done, 1)

            def norm_x_stats(a):
                dve.wait_ge(s_xa, a * 16 + 16)
                stats(ln_a, a, [xa[:, t, :] for t in range(T)])

            def norm_x(a):
                rstd(ln_a, a)
                dve.wait_ge(s_xtp, a * KE)
                norm_tiles(ln_a, xn, xa, s_xn)

            def split_x(a):
                for h in range(KE):
                    dve.wait_ge(s_xth, a * KE + h + 1)
                    nc.vector.tensor_tensor(xt_lo[:, h, :], wp[h][:], xt_hi[:, h, :].bitcast(F32), ALU.subtract
                                            ).then_inc(s_xtl, 1)

            def bias_kv(a, t):
                b = t % 2
                dve.wait_ge(s_kvp, a * T + t + 1)
                nc.vector.tensor_tensor(kv[:, b, :], wp[b][:], bkv_row[:], ALU.add).then_inc(s_kv, 1)

            def split_kv(a, t, pos):
                b = t % 2
                dve.wait_ge(s_hi, (a * T + t + 1) * 3)
                low(k_lo[:, b, :], kv[:, b, 0:E], k_hi[:, b, :].bitcast(F32), ALU.max).then_inc(s_lo, 1)
                v = kv[:, b, E:2 * E].rearrange("p (h c) -> p h c", h=KE)
                for s in range(2):
                    at = pos_cols[:, bass.ds(pos, 1), t, s:s + 1].rearrange("p o s -> p (o s)")
                    low(v_lo[:, b, :, s, 0:P], v, v_hi[:, b, :, s, 0:P].bitcast(F32), ALU.mult, at
                        ).then_inc(s_lo, 1)

            def head_matrices(b):
                dve.wait_ge(s_accz, b + 1)
                for h in range(KE):
                    nc.vector.tensor_copy(kv_sum[:, h].rearrange("p s c -> p (s c)"), acc[h][:, 0:2 * VW]
                                          ).then_inc(s_sum, 1)
                dve.wait_ge(s_sum, (b + 1) * KE)
                for g in range(G):
                    r0, h = (g % 2) * GW, g // 2
                    src = slice(r0, r0 + GW)
                    num = slice(r0, r0 + GW)
                    dn = slice(GW - r0, 2 * GW - r0)
                    for s in range(2):
                        o0 = r0 if s == 0 else GW - r0
                        dst = slice(o0, o0 + GW)
                        nc.vector.tensor_tensor(kvt[dst, g, num], kv_sum[src, h, s, r0:r0 + GW], mask[src, :],
                                                ALU.mult).then_inc(s_kvt, 1)
                        nc.vector.tensor_scalar(kvt[dst, g, dn], mask[src, :], kv_sum[src, h, s, P:P + 1], None,
                                                ALU.mult).then_inc(s_kvt, 1)
                dve.wait_ge(s_kvt, (b + 1) * 4 * G)
                dve.wait_ge(s_atp, b * NB * G)
                nc.vector.tensor_copy(kvt_hi[:], kvt[:]).then_inc(s_kvh, 1)
                dve.wait_ge(s_kvh, b + 1)
                nc.vector.tensor_tensor(kvt_lo[:], kvt[:], kvt_hi[:].bitcast(F32), ALU.subtract).then_inc(s_kvl, 1)

            def q_cos(c, pos):
                dve.wait_ge(s_rows, c * 16 + 16)
                dve.wait_ge(s_ql, c * G)
                for g in range(G):
                    r0 = (g % 2) * GW
                    nc.vector.tensor_tensor(qsc[GW - r0:2 * GW - r0, g, :],
                                            q_all[r0:r0 + GW, g // 2, bass.ds(pos * CH, CH)],
                                            pos_rows[r0:r0 + GW, 1, :], ALU.mult).then_inc(s_qc, 1)

            def split_q(c):
                for g in range(G):
                    dve.wait_ge(s_qh, c * G + g + 1)
                    nc.vector.tensor_tensor(qsc_lo[:, g, :], qsc[:, g, :], qsc_hi[:, g, :].bitcast(F32),
                                            ALU.subtract).then_inc(s_ql, 1)

            def divide(c, k):
                for g in (2 * k, 2 * k + 1):
                    r0 = (g % 2) * GW
                    dve.wait_ge(s_atp, c * G + g + 1)
                    nc.vector.tensor_scalar(att[r0:r0 + GW, k, :], wp[g % 2][GW - r0:2 * GW - r0, :], EPS_DEN, None,
                                            ALU.max).then_inc(s_den, 1)
                dve.wait_ge(s_den, c * G + 2 * k + 2)
                nc.vector.reciprocal(att[:, k, :], att[:, k, :]).then_inc(s_rden, 1)
                dve.wait_ge(s_rden, c * KE + k + 1)
                for g in (2 * k, 2 * k + 1):
                    r0 = (g % 2) * GW
                    nc.vector.tensor_tensor(att[r0:r0 + GW, k, :], wp[g % 2][r0:r0 + GW, :], att[r0:r0 + GW, k, :],
                                            ALU.mult).then_inc(s_att, 1)

            def split_att(c, k):
                dve.wait_ge(s_ath, c * KE + k + 1)
                nc.vector.tensor_tensor(att_lo[:, k, :], att[:, k, :], att_hi[:, k, :].bitcast(F32),
                                        ALU.subtract).then_inc(s_atl, 1)

            def bias_o(c):
                dve.wait_ge(s_x2p, c * KE)
                for i in range(2):
                    dve.wait_ge(s_op, c * 2 + i + 1)
                    nc.vector.tensor_tensor(ob[:, 2 * i:2 * i + 2, :], wp[i][:].rearrange("p (t e) -> p t e", t=2),
                                            bo_row[:].rearrange("p (o e) -> p o e", o=1).to_broadcast([P, 2, E]), ALU.add).then_inc(s_ob, 1)
                dve.wait_ge(s_ob, c * 2 + 2)
                stats(ln_o, c, [ob[:, t, :] for t in range(T)])

            def norm_o(c):
                rstd(ln_o, c)
                norm_tiles(ln_o, ob, ob, s_on)

            def stats_x1(c):
                dve.wait_ge(s_x1n, c + 1)
                stats(ln_2, c, [x1n[:, t, :] for t in range(T)])

            def norm_x1(c):
                rstd(ln_2, c)
                norm_tiles(ln_2, ob, x1n, s_xn2)

            def split_x2(c):
                for h in range(KE):
                    dve.wait_ge(s_x2h, c * KE + h + 1)
                    nc.vector.tensor_tensor(x2_lo[:, h, :], wp[h][:], x2_hi[:, h, :], ALU.subtract
                                            ).then_inc(s_x2l, 1)

            def hidden(f, n):
                dve.wait_ge(s_hh, f * 2 * KF + n + 1)
                hi, lo = (h1_hi, h1_lo) if n < KF else (h2_hi, h2_lo)
                low(lo[:, n % KF, :], ffp[n % 2][:], hi[:, n % KF, :], ALU.max).then_inc(s_hl, 1)

            def layer0(f):
                for n in range(KF):
                    hidden(f, n)

            def stats_y(f):
                stats(ln_f, f, [yp[t // 2][:, (t % 2) * E:(t % 2 + 1) * E] for t in range(T)],
                      lambda t: dve.wait_ge(s_yp, f * T + (t | 1) + 1))

            def norm_y(f):
                rstd(ln_f, f)
                nc.vector.tensor_scalar(ln_f.std[:], ln_f.rstd[:], ocs[:, 1:2], None, ALU.mult).then_inc(s_fc, 1)
                dve.wait_ge(s_fc, f + 1)
                nc.vector.scalar_tensor_tensor(out=ln_f.nmr[:], in0=ln_f.mean[:], scalar=-1.0, in1=ln_f.std[:],
                                               op0=ALU.mult, op1=ALU.mult).then_inc(ln_f.s_nmr, 1)

            nc.vector.memset(zero_l[:].bitcast(U32), 0).then_inc(s_zero, 1)
            nc.vector.memset(eps_col[:], EPS_LN).then_inc(s_zero, 1)
            norm_x_stats(0)
            norm_x(0)
            dve.wait_ge(s_first, 16 * FIRST_LOADS)
            nc.vector.tensor_copy(pos_hi[:], pos_cols[:]).then_inc(s_poshi, 1)
            dve.wait_ge(s_poshi, 1)
            nc.vector.tensor_tensor(pos_lo[:], pos_cols[:], pos_hi[:].bitcast(F32), ALU.subtract).then_inc(s_poslo, 1)
            for n, (lo, full, hi) in enumerate(((wkv_lo, wkv_f, wkv_hi), (wq_lo, wq_f, wq_hi))):
                dve.wait_ge(s_whi, n + 1)
                nc.vector.tensor_tensor(lo[:], full, hi[:].bitcast(F32), ALU.subtract).then_inc(s_wlo, 1)
            split_x(0)
            dve.wait_ge(s_whi, 3)
            nc.vector.tensor_tensor(wo_lo[:], wo_f, wo_hi[:].bitcast(F32), ALU.subtract).then_inc(s_wlo, 1)
            dve.wait_ge(s_late, 16 * LATE_LOADS)
            nc.vector.tensor_scalar(sgn[:], sv[:], 0.0, 2.0, ALU.is_ge, ALU.mult).then_inc(s_sc, 1)
            dve.wait_ge(s_sc, 1)
            nc.vector.tensor_scalar(sgn[:], sgn[:], -1.0, None, ALU.add).then_inc(s_sc, 1)
            dve.wait_ge(s_sc, 2)
            nc.vector.tensor_tensor(sab[:], sv[:], sgn[:], ALU.mult).then_inc(s_sc, 1)
            nc.vector.tensor_scalar(ksc[:, 0:1], sgn[:, 1:2], 2.0 * H1_SCALE, None, ALU.mult).then_inc(s_sc, 1)
            nc.vector.tensor_scalar(ksc[:, 1:2], sgn[:, 1:2], -H1_SCALE, None, ALU.mult).then_inc(s_sc, 1)
            dve.wait_ge(s_sc, 5)
            nc.vector.tensor_tensor(ocs[:, 0:1], sab[:, 0:1], sab[:, 1:2], ALU.mult).then_inc(s_sc, 1)
            dve.wait_ge(s_sc, 6)
            nc.vector.tensor_scalar(ocs[:, 1:2], ocs[:, 0:1], sv[:, 2:3], OUT_SCALE, ALU.mult, ALU.mult
                                    ).then_inc(s_sc, 1)
            dve.wait_ge(s_sc, 7)
            nc.vector.scalar_tensor_tensor(out=ocs[:, 2:3], in0=ocs[:, 1:2], scalar=1.0 / E, in1=ocs[:, 1:2],
                                           op0=ALU.mult, op1=ALU.mult).then_inc(s_sc, 1)
            dve.wait_ge(s_sc, 8)
            with dve.Fori(0, NB) as a:
                bias_kv(a, 0)
                bias_kv(a, 1)
                split_kv(a, 0, a)
                norm_x_stats(a + 1)
                bias_kv(a, 2)
                split_kv(a, 1, a)
                norm_x(a + 1)
                bias_kv(a, 3)
                split_kv(a, 2, a)
                split_kv(a, 3, a)
                split_x(a + 1)
            q_cos(0, 0)
            head_matrices(0)
            split_q(0)
            divide(0, 0)
            divide(0, 1)
            split_att(0, 0)
            split_att(0, 1)
            bias_o(0)
            norm_o(0)
            stats_x1(0)
            norm_x1(0)
            split_x2(0)
            with dve.Fori(0, NB - 1) as f:
                c, a, pos = f + 1, f + NB, f
                q_cos(c, c)
                layer0(f)
                split_q(c)
                divide(c, 0)
                hidden(f, 8)
                divide(c, 1)
                split_att(c, 0)
                hidden(f, 9)
                split_att(c, 1)
                hidden(f, 10)
                bias_o(c)
                norm_o(c)
                hidden(f, 11)
                bias_kv(a, 0)
                bias_kv(a, 1)
                split_kv(a, 0, pos)
                hidden(f, 12)
                stats_x1(c)
                bias_kv(a, 2)
                norm_x1(c)
                split_kv(a, 1, pos)
                norm_x_stats(a + 1)
                hidden(f, 13)
                bias_kv(a, 3)
                split_kv(a, 2, pos)
                norm_x(a + 1)
                hidden(f, 14)
                split_kv(a, 3, pos)
                split_x2(c)
                hidden(f, 15)
                split_x(a + 1)
                stats_y(f)
                norm_y(f)
            f = NB - 1
            c, a, pos = NB, NCH - 1, NB - 1
            layer0(f)
            bias_kv(a, 0)
            bias_kv(a, 1)
            split_kv(a, 0, pos)
            hidden(f, 8)
            bias_kv(a, 2)
            split_kv(a, 1, pos)
            hidden(f, 9)
            bias_kv(a, 3)
            split_kv(a, 2, pos)
            split_kv(a, 3, pos)
            hidden(f, 10)
            q_cos(c, 0)
            hidden(f, 11)
            head_matrices(1)
            split_q(c)
            hidden(f, 12)
            divide(c, 0)
            hidden(f, 13)
            divide(c, 1)
            split_att(c, 0)
            hidden(f, 14)
            split_att(c, 1)
            hidden(f, 15)
            bias_o(c)
            norm_o(c)
            stats_x1(c)
            norm_x1(c)
            stats_y(f)
            norm_y(f)
            split_x2(c)
            with dve.Fori(NB, NCH - 1) as f:
                c = f + 1
                q_cos(c, f - (NB - 1))
                layer0(f)
                split_q(c)
                divide(c, 0)
                hidden(f, 8)
                divide(c, 1)
                split_att(c, 0)
                hidden(f, 9)
                split_att(c, 1)
                hidden(f, 10)
                bias_o(c)
                norm_o(c)
                hidden(f, 11)
                hidden(f, 12)
                stats_x1(c)
                norm_x1(c)
                hidden(f, 13)
                hidden(f, 14)
                split_x2(c)
                hidden(f, 15)
                stats_y(f)
                norm_y(f)
            f = NCH - 1
            for n in range(2 * KF):
                hidden(f, n)
            stats_y(f)
            norm_y(f)

        @block.gpsimd
        def _(pool):
            def pos_in_v(a, pos):
                for t in range(T):
                    b = t % 2
                    if t < 2:
                        pool.wait_ge(s_acc, a * T)
                    else:
                        pool.wait_ge(s_acc, a * T + t - 1)
                    here = (slice(None), bass.ds(pos, 1), t, slice(None))
                    whole = pos_cols[here].to_broadcast([P, KE, 2])
                    for v, other in ((v_hi, pos_lo), (v_lo, pos_hi)):
                        part = other[:].bitcast(F32)[here].to_broadcast([P, KE, 2])
                        nc.gpsimd.tensor_tensor(v[:, b, :, :, P], whole, part, ALU.subtract).then_inc(s_pc, 1)

            def q_sin(c, pos, steps_of_a):
                if steps_of_a is not None:
                    pool.wait_ge(s_pc, steps_of_a * 2 * T)
                pool.wait_ge(s_rows, c * 16 + 16)
                pool.wait_ge(s_q, c * KE + KE)
                pool.wait_ge(s_ql, c * G)
                for g in range(G):
                    r0 = (g % 2) * GW
                    if g > 0:
                        pool.wait_ge(s_qs, c * G + g)
                    nc.gpsimd.tensor_tensor(qsc[r0:r0 + GW, g, :], q_all[r0:r0 + GW, g // 2, bass.ds(pos * CH, CH)],
                                            pos_rows[r0:r0 + GW, 0, :], ALU.mult).then_inc(s_qs, 1)

            def add_x(c):
                pool.wait_ge(s_xr, c * 16 + 16)
                pool.wait_ge(s_qs, c * G + G)
                pool.wait_ge(s_on, c * T + T)
                nc.gpsimd.tensor_tensor(x1n[:], ob[:], x1n[:], ALU.add).then_inc(s_x1n, 1)

            def add_x1(f):
                pool.wait_ge(s_fo, f * T + T)
                pool.wait_ge(s_x1, f + 1)
                nc.gpsimd.tensor_tensor(fo[:], fo[:], x1[:], ALU.add).then_inc(s_out, 1)
                pool.wait_ge(s_out, f + 1)

            pool.wait_ge(s_poslo, 1)
            pos_in_v(0, 0)
            pool.wait_ge(s_sc, 5)
            nc.gpsimd.tensor_scalar(w0_half, k0_u8, sgn[:, 0:1], 0.0, ALU.mult, ALU.add).then_inc(s_w0h, 1)
            pool.wait_ge(s_w0h, 1)
            nc.gpsimd.tensor_tensor(w0[:], w0_half[:, 0:KE], w0_half[:, KE:2 * KE], ALU.subtract).then_inc(s_ffw, 1)
            nc.gpsimd.tensor_scalar(w1[:], k1_u8, ksc[:, 0:1], ksc[:, 1:2], ALU.mult, ALU.add).then_inc(s_ffw, 1)
            nc.gpsimd.tensor_scalar(w2[:], k2_u8, 2.0, -1.0, ALU.mult, ALU.add).then_inc(s_ffw, 1)
            with pool.Fori(1, NB) as a:
                pos_in_v(a, a)
            pool.wait_ge(s_wlo, 3)
            q_sin(0, 0, NB)
            add_x(0)
            with pool.Fori(0, NB - 1) as f:
                q_sin(f + 1, f + 1, f + NB)
                add_x(f + 1)
                pos_in_v(f + NB, f)
                add_x1(f)
            f = NB - 1
            pos_in_v(NCH - 1, NB - 1)
            q_sin(NB, 0, NCH)
            add_x(NB)
            add_x1(f)
            with pool.Fori(NB, NCH - 1) as f:
                q_sin(f + 1, f - (NB - 1), None)
                add_x(f + 1)
                add_x1(f)
            add_x1(NCH - 1)


def kernel(L0_attn_x, L0_attn_Wq, L0_attn_bq, L0_attn_Wk, L0_attn_bk, L0_attn_Wv, L0_attn_bv, L0_attn_Wo,
           L0_attn_bo, L0_ffn_k0, L0_ffn_k1, L0_ffn_k2, L0_ffn_s0, L0_ffn_s1, L0_ffn_s2):
    import concourse.bacc as bacc
    from concourse.bass_utils import run_bass_kernel_spmd

    def a(v):
        return np.asarray(v)

    def rows(*v):
        return np.ascontiguousarray(np.concatenate([a(u).reshape(1, -1) for u in v], axis=1))

    pos_rows, pos_cols, ident, mask = shape_tables()
    arrays = {
        "x": np.ascontiguousarray(a(L0_attn_x).reshape(B * L, E)),
        "wq_t": np.ascontiguousarray(a(L0_attn_Wq).T),
        "wkv_t": np.ascontiguousarray(np.concatenate([a(L0_attn_Wk).T, a(L0_attn_Wv).T], axis=1)),
        "wo_t": np.ascontiguousarray(a(L0_attn_Wo).T),
        "bq": a(L0_attn_bq),
        "bkv": rows(L0_attn_bk, L0_attn_bv),
        "bo": rows(L0_attn_bo),
        "k0": np.ascontiguousarray(a(L0_ffn_k0)).view(np.uint32),
        "k1": np.ascontiguousarray(a(L0_ffn_k1)).view(np.uint32),
        "k2": np.ascontiguousarray(a(L0_ffn_k2)).view(np.uint32),
        "s0": a(L0_ffn_s0).reshape(1, 1),
        "s1": a(L0_ffn_s1).reshape(1, 1),
        "s2": a(L0_ffn_s2).reshape(1, 1),
        "pos_rows_in": pos_rows, "pos_cols_in": pos_cols, "ident_in": ident, "mask_in": mask,
    }
    nc = bacc.Bacc("TRN2", target_bir_lowering=False, num_devices=1)
    d = {n: nc.dram_tensor(n, list(v.shape), mybir.dt.from_np(v.dtype), kind="ExternalInput").ap()
         for n, v in arrays.items()}
    out = nc.dram_tensor("out", [B * L, E], F32, kind="ExternalOutput").ap()
    build(nc, d["x"], d["wq_t"], d["wkv_t"], d["wo_t"], d["bq"], d["bkv"], d["bo"], d["k0"], d["k1"], d["k2"],
          (d["s0"], d["s1"], d["s2"]), d["pos_rows_in"], d["pos_cols_in"], d["ident_in"], d["mask_in"], out)
    r = run_bass_kernel_spmd(nc, [arrays], core_ids=[0])
    return r.results[0]["out"].reshape(B, L, E)
```

```python
from contextlib import ExitStack

import numpy as np

import concourse.bass as bass
from concourse import mybir

F32 = mybir.dt.float32
F32R = mybir.dt.float32r
F16 = mybir.dt.float16
U8 = mybir.dt.uint8
U32 = mybir.dt.uint32
ALU = mybir.AluOpType
ACT = mybir.ActivationFunctionType

P = 128
B, L, E = 2, 4096, 256
HEADS = 16
HD = E // HEADS
F = 1024
T = 4
CH = T * P
NB = L // CH
NCH = B * NB
KE = E // P
KF = F // P
G = 4
GW = E // G
VW = P + 1
EPS_DEN = 1e-4
EPS_LN = 1e-5
H1_SCALE = 2.0 ** -4
OUT_SCALE = 8.0 / H1_SCALE


def shape_tables():
    idx = (np.float32(np.pi / 2) * np.arange(1, L + 1, dtype=np.float32) / np.float32(L)).astype(np.float32)
    sc = np.stack([np.sin(idx), np.cos(idx)]).astype(np.float32)
    by = sc.reshape(2, NB, P, T)
    rows = np.tile(by.transpose(1, 0, 3, 2).reshape(NB, 2 * CH), (B, 1))
    cols = np.ascontiguousarray(by.transpose(2, 1, 3, 0)).reshape(P, NB * T * 2)
    ident = np.eye(P, dtype=np.float32)
    r, c = np.arange(P)[:, None] % GW, np.arange(GW)[None, :]
    mask = (r // HD == c // HD).astype(np.float32)
    return rows, cols, ident, mask


def build(nc, x, wq_t, wkv_t, wo_t, bq, bkv, bo, k0, k1, k2, scales, rows_d, cols_d, ident_d, mask_d, out):
    ctx = ExitStack()
    with ctx:
        def sb(name, shape, dt=F32):
            return ctx.enter_context(nc.sbuf_tensor(name, shape, dt))

        def sem(name):
            return ctx.enter_context(nc.semaphore(name))

        ident = sb("ident", [P, P])
        mask = sb("mask", [P, GW])
        pos_cols = sb("pos_cols", [P, NB, T, 2])
        pos_hi = sb("pos_hi", [P, NB, T, 2], F32R)
        pos_lo = sb("pos_lo", [P, NB, T, 2], F32R)
        wq_hi = sb("wq_hi", [P, KE, E], F32R)
        wq_lo = sb("wq_lo", [P, KE, E], F32R)
        wkv_hi = sb("wkv_hi", [P, KE, 2 * E], F32R)
        wkv_lo = sb("wkv_lo", [P, KE, 2 * E], F32R)
        wo_hi = sb("wo_hi", [P, KE, E], F32R)
        wo_lo = sb("wo_lo", [P, KE, E], F32R)
        bq_col = sb("bq_col", [P, KE])
        bkv_row = sb("bkv_row", [P, 2 * E])
        bo_row = sb("bo_row", [P, E])
        w0 = sb("w0", [P, KE, F], F16)
        w1 = sb("w1", [P, KF, F], F16)
        w2 = sb("w2", [P, KF, E], F16)
        sv = sb("sv", [P, 3])
        sgn = sb("sgn", [P, 3])
        sab = sb("sab", [P, 3])
        ksc = sb("ksc", [P, 4])
        ocs = sb("ocs", [P, 3])

        xa = sb("xa", [P, T, E])
        xn = sb("xn", [P, T, E])
        xt_hi = sb("xt_hi", [P, KE, CH], F32R)
        xt_lo = sb("xt_lo", [P, KE, CH], F32R)
        q_all = sb("q_all", [P, KE, L])
        kv = sb("kv", [P, 2, 2 * E])
        k_hi = sb("k_hi", [P, 2, E], F32R)
        k_lo = sb("k_lo", [P, 2, E], F32R)
        v_hi = sb("v_hi", [P, 2, KE, 2, VW], F32R)
        v_lo = sb("v_lo", [P, 2, KE, 2, VW], F32R)
        eps_col = sb("eps_col", [P, 1])
        zero_l = sb("zero_l", [P, P], F32R)
        kvt_hi = sb("kvt_hi", [P, G, P], F32R)
        kvt_lo = sb("kvt_lo", [P, G, P], F32R)

        pos_rows = sb("pos_rows", [P, 2, CH])
        qsc = sb("qsc", [P, G, CH])
        qsc_hi = sb("qsc_hi", [P, G, CH], F32R)
        qsc_lo = sb("qsc_lo", [P, G, CH], F32R)
        att = sb("att", [P, KE, CH])
        att_hi = sb("att_hi", [P, KE, CH], F32R)
        att_lo = sb("att_lo", [P, KE, CH], F32R)
        x1n = sb("x1n", [P, T, E])
        ob = sb("ob", [P, T, E])
        x1 = sb("x1", [P, T, E])
        kv_sum = ob[:].rearrange("p t e -> p (t e)")[:, 0:KE * 2 * VW].rearrange("p (h s c) -> p h s c", h=KE, s=2)
        kvt = att[:, 0, :].rearrange("p (g m) -> p g m", g=G)
        x2_hi = sb("x2_hi", [P, KE, CH], F16)
        x2_lo = sb("x2_lo", [P, KE, CH], F16)
        h1_hi = sb("h1_hi", [P, KF, CH], F16)
        h1_lo = sb("h1_lo", [P, KF, CH], F16)
        h2_hi = sb("h2_hi", [P, KF, CH], F16)
        h2_lo = sb("h2_lo", [P, KF, CH], F16)
        fo = sb("fo", [P, T, E])

        wq_f = qsc[:, 0, :].rearrange("p (k e) -> p k e", k=KE)
        wo_f = qsc[:, 1, :].rearrange("p (k e) -> p k e", k=KE)
        wkv_f = qsc[:, 2:4, :]
        k1_u8 = h1_hi[:].bitcast(U8).rearrange("p k c -> p (k c)").rearrange("p (k f) -> p k f", k=KF)
        k0_u8 = h1_lo[:].bitcast(U8).rearrange("p k c -> p (k c)")[:, 0:4 * F].rearrange("p (k f) -> p k f", k=4)
        k2_u8 = h1_lo[:].bitcast(U8).rearrange("p k c -> p (k c)")[:, 4 * F:4 * F + KF * E].rearrange(
            "p (k f) -> p k f", k=KF)
        w0_half = h2_hi[:].rearrange("p k c -> p (k c)").rearrange("p (k f) -> p k f", k=4)

        class Norm:

            def __init__(self, name):
                self.stats = sb(name + "_stats", [P, T, 6])
                self.d = sb(name + "_d", [P, 4, T])
                self.var = sb(name + "_var", [P, T])
                self.std = sb(name + "_std", [P, T])
                self.rstd = sb(name + "_rstd", [P, T])
                self.nmr = sb(name + "_nmr", [P, T])
                self.s_stats = sem(name + "_stats_done")
                self.s_d = sem(name + "_d_done")
                self.s_d2 = sem(name + "_d2_done")
                self.s_var = sem(name + "_var_done")
                self.s_std = sem(name + "_std_done")
                self.s_rstd = sem(name + "_rstd_done")
                self.s_nmr = sem(name + "_nmr_done")

        ln_a, ln_o, ln_2, ln_f = Norm("ln_a"), Norm("ln_o"), Norm("ln_2"), Norm("ln_f")

        def bank(name):
            return ctx.enter_context(nc.psum_tensor(name, [P, 512], F32))

        acc = [bank("acc0"), bank("acc1")]
        ffp = [bank("ffp0"), bank("ffp1")]
        yp = [bank("yp0"), bank("yp1")]
        wp = [bank("wp0"), bank("wp1")]

        wide = [ffp[0], ffp[1], yp[0], yp[1]]

        s_first = sem("first_loads")
        s_late = sem("late_loads")
        s_xa = sem("xa_loaded")
        s_xr = sem("xr_loaded")
        s_rows = sem("pos_rows_loaded")
        s_free = sem("fo_free")
        s_whi = sem("w_hi_ready")
        s_wlo = sem("w_lo_ready")
        s_zero = sem("zero_ready")
        s_poshi = sem("pos_hi_ready")
        s_poslo = sem("pos_lo_ready")
        s_sc = sem("scale_terms")
        s_w0h = sem("w0_halves")
        s_ffw = sem("ffn_weights_ready")

        s_xn = sem("xn_ready")
        s_xtp = sem("xt_in_psum")
        s_xth = sem("xt_hi_ready")
        s_xtl = sem("xt_lo_ready")
        s_qp = sem("q_in_psum")
        s_q = sem("q_kept")
        s_kvp = sem("kv_in_psum")
        s_kv = sem("kv_biased")
        s_hi = sem("kv_hi_ready")
        s_lo = sem("kv_lo_ready")
        s_pc = sem("pos_in_v")
        s_acc = sem("acc_step_done")
        s_accz = sem("acc_closed")
        s_sum = sem("kv_sum_ready")
        s_kvz = sem("kvt_cleared")
        s_kvt = sem("kvt_ready")
        s_kvh = sem("kvt_hi_ready")
        s_kvl = sem("kvt_lo_ready")

        s_qs = sem("q_sin_ready")
        s_qc = sem("q_cos_ready")
        s_qh = sem("qsc_hi_ready")
        s_ql = sem("qsc_lo_ready")
        s_atp = sem("att_in_psum")
        s_den = sem("den_ready")
        s_rden = sem("rden_ready")
        s_att = sem("att_ready")
        s_ath = sem("att_hi_ready")
        s_atl = sem("att_lo_ready")
        s_op = sem("o_in_psum")
        s_ob = sem("o_biased")
        s_on = sem("o_normed")
        s_x1n = sem("x1n_ready")
        s_x1 = sem("x1_kept")
        s_xn2 = sem("xn2_ready")
        s_x2p = sem("x2_in_psum")
        s_x2h = sem("x2_hi_ready")
        s_x2l = sem("x2_lo_ready")

        s_hp = sem("h_in_psum")
        s_hh = sem("h_hi_ready")
        s_hl = sem("h_lo_ready")
        s_yp = sem("y_in_psum")
        s_fc = sem("f_scale_ready")
        s_fo = sem("f_normed")
        s_out = sem("out_ready")

        x_c = x.rearrange("(c p t) e -> c p (t e)", p=P, t=T)
        out_c = out.rearrange("(c p t) e -> c p (t e)", p=P, t=T)

        def after(eng, s, count):
            if not isinstance(count, int) or count > 0:
                eng.wait_ge(s, count)

        def pick(ap, i):
            return ap[bass.ds(i, 1)].rearrange("o p f -> (o p) f")

        FIRST_LOADS, LATE_LOADS = 8, 9
        block = ctx.enter_context(nc.Block())

        @block.sync
        def _(sp):
            def load_x(a):
                src = pick(x_c, a)
                sp.wait_ge(s_xn, a * T)
                sp.dma_start(xa[:].rearrange("p t e -> p (t e)"), src).then_inc(s_xa, 16)

            def load_rows(c):
                src = rows_d[bass.ds(c, 1), :].to_broadcast([P, 2 * CH])
                after(sp, s_qs, c * G)
                after(sp, s_qc, c * G)
                sp.dma_start(pos_rows[:].rearrange("p s c -> p (s c)"), src).then_inc(s_rows, 16)

            def load_xr(c):
                src = pick(x_c, c)
                after(sp, s_x1, c)
                sp.dma_start(x1n[:].rearrange("p t e -> p (t e)"), src).then_inc(s_xr, 16)

            def store(f):
                dst = pick(out_c, f)
                sp.wait_ge(s_out, f + 2)
                sp.dma_start(dst, fo[:].rearrange("p t e -> p (t e)")).then_inc(s_free, 16)

            sp.dma_start(xa[:].rearrange("p t e -> p (t e)"), x_c[0]).then_inc(s_xa, 16)
            sp.dma_start(ident[:], ident_d).then_inc(s_first, 16)
            sp.dma_start(wkv_f, wkv_t.rearrange("(k p) f -> p k f", p=P)).then_inc(s_first, 16)
            sp.dma_start(wq_f, wq_t.rearrange("(k p) f -> p k f", p=P)).then_inc(s_first, 16)
            sp.dma_start(wo_f, wo_t.rearrange("(k p) f -> p k f", p=P)).then_inc(s_first, 16)
            sp.dma_start(bq_col[:], bq.rearrange("(k p) -> p k", p=P), allow_slow_non_contiguous=True).then_inc(s_first, 16)
            sp.dma_start(bkv_row[:], bkv.to_broadcast([P, 2 * E])).then_inc(s_first, 16)
            sp.dma_start(bo_row[:], bo.to_broadcast([P, E])).then_inc(s_first, 16)
            sp.dma_start(pos_cols[:].rearrange("p c t s -> p (c t s)"), cols_d).then_inc(s_first, 16)
            sp.dma_start(mask[:], mask_d).then_inc(s_late, 16)
            for n in range(3):
                sp.dma_start(sv[:, n:n + 1], scales[n].to_broadcast([P, 1]),
                             allow_slow_non_contiguous=True).then_inc(s_late, 16)
            sp.dma_start(k0_u8.bitcast(U32), k0.rearrange("(k p) f -> p k f", p=P)).then_inc(s_late, 16)
            half = KF // 2
            sp.dma_start(k1_u8[:, 0:half].bitcast(U32), k1[0:half * P].rearrange("(k p) f -> p k f", p=P)).then_inc(s_late, 16)
            sp.dma_start(k1_u8[:, half:KF].bitcast(U32), k1[half * P:F].rearrange("(k p) f -> p k f", p=P)).then_inc(s_late, 16)
            sp.dma_start(k2_u8[:, 0:half].bitcast(U32), k2[0:half * P].rearrange("(k p) f -> p k f", p=P)).then_inc(s_late, 16)
            sp.dma_start(k2_u8[:, half:KF].bitcast(U32), k2[half * P:F].rearrange("(k p) f -> p k f", p=P)).then_inc(s_late, 16)
            load_rows(0)
            load_xr(0)
            with sp.Fori(1, NB + 1) as a:
                load_x(a)
            load_rows(1)
            load_x(NB + 1)
            with sp.Fori(0, NB - 2) as f:
                load_x(f + (NB + 2))
                load_xr(f + 1)
                load_rows(f + 2)
                store(f)
            with sp.Fori(NB - 2, NCH - 2) as f:
                load_xr(f + 1)
                load_rows(f + 2)
                store(f)
            load_xr(NCH - 1)
            store(NCH - 2)
            store(NCH - 1)
            sp.wait_ge(s_free, 16 * (NCH + 1))

        @block.tensor
        def _(pe):
            def mm(dst, lhs, rhs, start, stop):
                return nc.tensor.matmul(dst, lhs, rhs, start=start, stop=stop)

            def passes(dst, pairs, acc_open=False):
                last = None
                n = 0
                for (lh, ll), (rh, rl) in pairs:
                    for u, v in ((lh, rh), (lh, rl), (ll, rh)):
                        last = mm(dst, u, v, n == 0 and not acc_open, n == 3 * len(pairs) - 1 and not acc_open)
                        n += 1
                return last

            def transpose_x(a):
                pe.wait_ge(s_xn, a * T + T)
                for h in range(KE):
                    for t in range(T):
                        last = nc.tensor.transpose(wp[h][:, t * P:(t + 1) * P], xn[:, t, h * P:(h + 1) * P], ident[:])
                    last.then_inc(s_xtp, 1)

            def project_q(a):
                pe.wait_ge(s_xtl, a * KE + KE)
                for h in range(KE):
                    m = slice(h * P, (h + 1) * P)
                    passes(wp[h][:], [((wq_hi[:, k, m], wq_lo[:, k, m]), (xt_hi[:, k, :], xt_lo[:, k, :]))
                                      for k in range(KE)]).then_inc(s_qp, 1)

            def project_kv(a, t, banks):
                if t >= len(banks):
                    pe.wait_ge(s_kv, a * T + t - len(banks) + 1)
                m = slice(t * P, (t + 1) * P)
                passes(banks[t % len(banks)][:], [((xt_hi[:, k, m], xt_lo[:, k, m]), (wkv_hi[:, k, :], wkv_lo[:, k, :]))
                                      for k in range(KE)]).then_inc(s_kvp, 1)

            def sum_kv(a, t):
                pe.wait_ge(s_lo, (a * T + t + 1) * 3)
                pe.wait_ge(s_pc, (a * T + t + 1) * 2)
                b = t % 2
                for h in range(KE):
                    m = slice(h * P, (h + 1) * P)
                    last = passes(acc[h][:, 0:2 * VW], [((k_hi[:, b, m], k_lo[:, b, m]),
                                  (v_hi[:, b, h].rearrange("p s c -> p (s c)"),
                                   v_lo[:, b, h].rearrange("p s c -> p (s c)")))], acc_open=True)
                last.then_inc(s_acc, 1)

            def open_acc():
                for h in range(KE):
                    mm(acc[h][:, 0:2 * VW], zero_l[:], wkv_hi[:, 0, 0:2 * VW], True, False)

            def close_acc():
                for h in range(KE):
                    last = mm(acc[h][:, 0:2 * VW], zero_l[:], wkv_hi[:, 0, 0:2 * VW], False, True)
                last.then_inc(s_accz, 1)

            def attend(c, g):
                pe.wait_ge(s_ql, c * G + g + 1)
                if g >= 2:
                    pe.wait_ge(s_att, c * G + g - 1)
                passes(wp[g % 2][:], [((kvt_hi[:, g, :], kvt_lo[:, g, :]), (qsc_hi[:, g, :], qsc_lo[:, g, :]))]
                       ).then_inc(s_atp, 1)

            def project_o(c):
                pe.wait_ge(s_atl, c * KE + KE)
                for t in range(T):
                    m = slice(t * P, (t + 1) * P)
                    last = passes(wp[t // 2][:, (t % 2) * E:(t % 2 + 1) * E],
                                  [((att_hi[:, k, m], att_lo[:, k, m]), (wo_hi[:, k, :], wo_lo[:, k, :]))
                                   for k in range(KE)])
                    if t % 2:
                        last.then_inc(s_op, 1)

            def transpose_x2(c):
                pe.wait_ge(s_xn2, c * T + T)
                for h in range(KE):
                    for t in range(T):
                        last = nc.tensor.transpose(wp[h][:, t * P:(t + 1) * P], ob[:, t, h * P:(h + 1) * P], ident[:])
                    last.then_inc(s_x2p, 1)

            def hidden(f, n, w, hi, lo, kn):
                j = n % KF
                if n >= 2:
                    pe.wait_ge(s_hl, f * 2 * KF + n - 1)
                m = slice(j * P, (j + 1) * P)
                for k in range(kn):
                    mm(ffp[n % 2][:], w[:, k, m], hi[:, k, :], k == 0, False)
                    last = mm(ffp[n % 2][:], w[:, k, m], lo[:, k, :], False, k == kn - 1)
                last.then_inc(s_hp, 1)

            def layer0(f):
                pe.wait_ge(s_x2l, f * KE + KE)
                for j in range(KF):
                    hidden(f, j, w0, x2_hi, x2_lo, KE)

            def layer1(f, j):
                if j == 0:
                    pe.wait_ge(s_hl, f * 2 * KF + KF)
                hidden(f, KF + j, w1, h1_hi, h1_lo, KF)

            def layer2(f, t):
                if t == 0:
                    pe.wait_ge(s_hl, (f + 1) * 2 * KF)
                m = slice(t * P, (t + 1) * P)
                dst = yp[t // 2][:, (t % 2) * E:(t % 2 + 1) * E]
                for k in range(KF):
                    mm(dst, h2_hi[:, k, m], w2[:, k, :], k == 0, False)
                    last = mm(dst, h2_lo[:, k, m], w2[:, k, :], False, k == KF - 1)
                last.then_inc(s_yp, 1)

            pe.wait_ge(s_first, 16 * FIRST_LOADS)
            transpose_x(0)
            pe.wait_ge(s_wlo, 3)
            pe.wait_ge(s_zero, 1)
            open_acc()
            with pe.Fori(0, NB) as a:
                project_q(a)
                for t in range(T):
                    project_kv(a, t, wide)
                pe.wait_ge(s_q, a * KE + KE)
                transpose_x(a + 1)
                for t in range(T):
                    sum_kv(a, t)
            close_acc()
            project_q(NB)
            for t in range(T):
                project_kv(NB, t, wide)
            pe.wait_ge(s_q, NB * KE + KE)
            pe.wait_ge(s_kvl, 1)
            attend(0, 0)
            attend(0, 1)
            open_acc()
            attend(0, 2)
            attend(0, 3)
            sum_kv(NB, 0)
            sum_kv(NB, 1)
            project_o(0)
            sum_kv(NB, 2)
            sum_kv(NB, 3)
            pe.wait_ge(s_ob, 2)
            transpose_x(NB + 1)
            pe.wait_ge(s_xtl, (NB + 1) * KE + KE)
            transpose_x2(0)
            pe.wait_ge(s_ffw, 3)
            layer0(0)

            def both(f, last):
                c, a = f + 1, f + (NB + 1)
                attend(c, 0)
                attend(c, 1)
                layer1(f, 0)
                pe.wait_ge(s_fo, f * T + T)
                project_kv(a, 0, yp)
                project_kv(a, 1, yp)
                layer1(f, 1)
                attend(c, 2)
                attend(c, 3)
                sum_kv(a, 0)
                project_kv(a, 2, yp)
                layer1(f, 2)
                sum_kv(a, 1)
                project_kv(a, 3, yp)
                layer1(f, 3)
                project_o(c)
                sum_kv(a, 2)
                layer1(f, 4)
                sum_kv(a, 3)
                layer1(f, 5)
                pe.wait_ge(s_ob, c * 2 + 2)
                project_q(a)
                layer1(f, 6)
                layer1(f, 7)
                pe.wait_ge(s_q, a * KE + KE)
                transpose_x2(c)
                pe.wait_ge(s_kv, a * T + T)
                layer2(f, 0)
                layer2(f, 1)
                if not last:
                    pe.wait_ge(s_x2l, c * KE + KE)
                    transpose_x(a + 1)
                else:
                    close_acc()
                layer2(f, 2)
                layer2(f, 3)
                layer0(f + 1)

            def ff_at(f):
                c = f + 1
                attend(c, 0)
                attend(c, 1)
                layer1(f, 0)
                layer1(f, 1)
                attend(c, 2)
                attend(c, 3)
                layer1(f, 2)
                layer1(f, 3)
                project_o(c)
                for j in range(4, KF):
                    layer1(f, j)
                layer2(f, 0)
                transpose_x2(c)
                for t in range(1, T):
                    layer2(f, t)
                layer0(f + 1)

            with pe.Fori(0, NB - 2) as f:
                both(f, False)
            both(NB - 2, True)
            pe.wait_ge(s_kvl, 2)
            with pe.Fori(NB - 1, NCH - 1) as f:
                ff_at(f)
            f = NCH - 1
            for j in range(KF):
                layer1(f, j)
            for t in range(T):
                layer2(f, t)

        @block.scalar
        def _(act):
            def std(ln, n, scale=1.0 / E):
                act.wait_ge(ln.s_var, n + 1)
                nc.scalar.activation(ln.std[:], ln.var[:], ACT.Sqrt, bias=eps_col[:], scale=scale
                                     ).then_inc(ln.s_std, 1)

            def norm(ln, n, dst, src, done):
                act.wait_ge(ln.s_nmr, n + 1)
                for t in range(T):
                    nc.scalar.activation(dst[:, t, :], src[:, t, :], ACT.Identity, bias=ln.nmr[:, t:t + 1],
                                         scale=ln.rstd[:, t:t + 1]).then_inc(done, 1)

            def norm_x(a):
                after(act, s_xtp, a * KE)
                norm(ln_a, a, xn, xa, s_xn)

            def split_x(a):
                for h in range(KE):
                    act.wait_ge(s_xtp, a * KE + h + 1)
                    nc.scalar.activation(xt_hi[:, h, :], wp[h][:], ACT.Copy).then_inc(s_xth, 1)

            def keep_q(a, pos):
                for h in range(KE):
                    act.wait_ge(s_qp, a * KE + h + 1)
                    nc.scalar.activation(q_all[:, h, bass.ds(pos * CH, CH)], wp[h][:], ACT.Relu,
                                         bias=bq_col[:, h:h + 1]).then_inc(s_q, 1)

            def split_kv(a, t, pos):
                b = t % 2
                act.wait_ge(s_kv, a * T + t + 1)
                if t >= 2:
                    act.wait_ge(s_acc, a * T + t - 1)
                nc.scalar.activation(k_hi[:, b, :], kv[:, b, 0:E], ACT.Relu).then_inc(s_hi, 1)
                v = kv[:, b, E:2 * E].rearrange("p (h c) -> p h c", h=KE)
                for s in range(2):
                    at = pos_cols[:, bass.ds(pos, 1), t, s:s + 1].rearrange("p o s -> p (o s)")
                    nc.scalar.activation(v_hi[:, b, :, s, 0:P], v, ACT.Copy, scale=at).then_inc(s_hi, 1)

            def split_q(c):
                for g in range(G):
                    act.wait_ge(s_qs, c * G + g + 1)
                    act.wait_ge(s_qc, c * G + g + 1)
                    if g == 0:
                        after(act, s_atp, c * G)
                    nc.scalar.activation(qsc_hi[:, g, :], qsc[:, g, :], ACT.Copy).then_inc(s_qh, 1)

            def split_att(c, k):
                act.wait_ge(s_att, c * G + 2 * k + 2)
                after(act, s_op, c * 2)
                nc.scalar.activation(att_hi[:, k, :], att[:, k, :], ACT.Copy).then_inc(s_ath, 1)

            def split_x2(c):
                for h in range(KE):
                    act.wait_ge(s_x2p, c * KE + h + 1)
                    nc.scalar.activation(x2_hi[:, h, :], wp[h][:], ACT.Copy).then_inc(s_x2h, 1)

            def hidden(f, n):
                act.wait_ge(s_hp, f * 2 * KF + n + 1)
                dst = (h1_hi if n < KF else h2_hi)[:, n % KF, :]
                nc.scalar.activation(dst, ffp[n % 2][:], ACT.Relu).then_inc(s_hh, 1)

            def layer0(f):
                for n in range(KF):
                    hidden(f, n)

            def keep_x1(f):
                act.wait_ge(s_x1n, f + 1)
                act.wait_ge(s_out, f + 1)
                nc.scalar.copy(x1[:], x1n[:]).then_inc(s_x1, 1)

            def norm_y(f):
                act.wait_ge(ln_f.s_nmr, f + 1)
                act.wait_ge(s_free, f * 16 + 16)
                for t in range(T):
                    nc.scalar.activation(fo[:, t, :], yp[t // 2][:, (t % 2) * E:(t % 2 + 1) * E], ACT.Identity,
                                         bias=ln_f.nmr[:, t:t + 1], scale=ln_f.std[:, t:t + 1]).then_inc(s_fo, 1)

            act.sem_inc(s_free, 16)
            act.sem_inc(s_fo, T)
            act.wait_ge(s_zero, 2)
            act.wait_ge(s_first, 16 * FIRST_LOADS)
            std(ln_a, 0)
            nc.scalar.activation(wkv_hi[:], wkv_f, ACT.Copy).then_inc(s_whi, 1)
            norm_x(0)
            nc.scalar.activation(wq_hi[:], wq_f, ACT.Copy).then_inc(s_whi, 1)
            split_x(0)
            nc.scalar.activation(wo_hi[:], wo_f, ACT.Copy).then_inc(s_whi, 1)
            with act.Fori(0, NB) as a:
                keep_q(a, a)
                std(ln_a, a + 1)
                norm_x(a + 1)
                for t in range(T):
                    split_kv(a, t, a)
                split_x(a + 1)
            split_q(0)
            keep_q(NB, 0)
            split_kv(NB, 0, 0)
            split_kv(NB, 1, 0)
            split_att(0, 0)
            split_kv(NB, 2, 0)
            split_att(0, 1)
            split_kv(NB, 3, 0)
            std(ln_a, NB + 1)
            norm_x(NB + 1)
            std(ln_o, 0)
            norm(ln_o, 0, ob, ob, s_on)
            split_x(NB + 1)
            split_q(1)
            std(ln_2, 0)
            norm(ln_2, 0, ob, x1n, s_xn2)
            split_x2(0)
            layer0(0)

            def both(f, pos, last):
                c, a = f + 1, f + (NB + 1)
                keep_x1(f)
                hidden(f, 8)
                split_att(c, 0)
                split_kv(a, 0, pos)
                split_kv(a, 1, pos)
                hidden(f, 9)
                hidden(f, 10)
                split_kv(a, 2, pos)
                split_att(c, 1)
                split_kv(a, 3, pos)
                hidden(f, 11)
                if not last:
                    std(ln_a, a + 1)
                    norm_x(a + 1)
                std(ln_o, c)
                norm(ln_o, c, ob, ob, s_on)
                hidden(f, 12)
                hidden(f, 13)
                keep_q(a, pos)
                std(ln_2, c)
                norm(ln_2, c, ob, x1n, s_xn2)
                hidden(f, 14)
                split_q(c + 1)
                hidden(f, 15)
                split_x2(c)
                if not last:
                    split_x(a + 1)
                layer0(f + 1)
                std(ln_f, f, ocs[:, 2:3])
                norm_y(f)

            def ff_at(f, next_q):
                c = f + 1
                keep_x1(f)
                hidden(f, 8)
                split_att(c, 0)
                hidden(f, 9)
                hidden(f, 10)
                split_att(c, 1)
                hidden(f, 11)
                std(ln_o, c)
                norm(ln_o, c, ob, ob, s_on)
                hidden(f, 12)
                hidden(f, 13)
                std(ln_2, c)
                norm(ln_2, c, ob, x1n, s_xn2)
                hidden(f, 14)
                if next_q:
                    split_q(c + 1)
                hidden(f, 15)
                split_x2(c)
                layer0(f + 1)
                std(ln_f, f, ocs[:, 2:3])
                norm_y(f)

            with act.Fori(0, NB - 2) as f:
                both(f, f + 1, False)
            both(NB - 2, NB - 1, True)
            with act.Fori(NB - 1, NCH - 2) as f:
                ff_at(f, True)
            ff_at(NCH - 2, False)
            f = NCH - 1
            keep_x1(f)
            for n in range(KF, 2 * KF):
                hidden(f, n)
            std(ln_f, f, ocs[:, 2:3])
            norm_y(f)

        @block.vector
        def _(dve):
            def low(dst, src, hi, sign_op=None, scalar=0.0):
                return nc.vector.scalar_tensor_tensor(out=dst, in0=src, scalar=scalar, in1=hi,
                                                      op0=sign_op, op1=ALU.subtract)

            def moments(ln, tiles, ts=range(T)):
                for t in ts:
                    nc.vector.bn_stats(ln.stats[:, t, :], tiles[t]).then_inc(ln.s_stats, 1)

            def variance(ln, n):
                dve.wait_ge(ln.s_stats, n * T + T)
                even, odd = ln.stats[:, :, 1], ln.stats[:, :, 4]
                nc.vector.tensor_tensor(ln.d[:, 1, :], even, odd, ALU.subtract).then_inc(ln.s_d, 1)
                nc.vector.tensor_tensor(ln.d[:, 2, :], ln.stats[:, :, 2], ln.stats[:, :, 5], ALU.add
                                        ).then_inc(ln.s_d, 1)
                nc.vector.tensor_tensor(ln.d[:, 0, :], even, odd, ALU.add).then_inc(ln.s_d, 1)
                dve.wait_ge(ln.s_d, n * 3 + 3)
                nc.vector.tensor_tensor(ln.d[:, 3, :], ln.d[:, 1, :], ln.d[:, 1, :], ALU.mult).then_inc(ln.s_d2, 1)
                dve.wait_ge(ln.s_d2, n + 1)
                nc.vector.scalar_tensor_tensor(out=ln.var[:], in0=ln.d[:, 3, :], scalar=E / 4.0, in1=ln.d[:, 2, :],
                                               op0=ALU.mult, op1=ALU.add).then_inc(ln.s_var, 1)

            def stats(ln, n, tiles):
                moments(ln, tiles)
                variance(ln, n)

            def rstd(ln, n):
                dve.wait_ge(ln.s_std, n + 1)
                nc.vector.reciprocal(ln.rstd[:], ln.std[:]).then_inc(ln.s_rstd, 1)
                dve.wait_ge(ln.s_rstd, n + 1)

            def shift(ln, n, by):
                nc.vector.scalar_tensor_tensor(out=ln.nmr[:], in0=ln.d[:, 0, :], scalar=-0.5, in1=by,
                                               op0=ALU.mult, op1=ALU.mult).then_inc(ln.s_nmr, 1)

            def scale_shift(ln, n):
                rstd(ln, n)
                shift(ln, n, ln.rstd[:])

            def norm_x_stats(a):
                dve.wait_ge(s_xa, a * 16 + 16)
                stats(ln_a, a, [xa[:, t, :] for t in range(T)])

            def split_x(a):
                for h in range(KE):
                    dve.wait_ge(s_xth, a * KE + h + 1)
                    nc.vector.tensor_tensor(xt_lo[:, h, :], wp[h][:], xt_hi[:, h, :].bitcast(F32), ALU.subtract
                                            ).then_inc(s_xtl, 1)

            def bias_kv(a, t, banks):
                b = t % 2
                if t >= 2:
                    dve.wait_ge(s_lo, (a * T + t - 1) * 3)
                dve.wait_ge(s_kvp, a * T + t + 1)
                nc.vector.tensor_tensor(kv[:, b, :], banks[t % len(banks)][:], bkv_row[:], ALU.add).then_inc(s_kv, 1)

            def split_kv(a, t, pos):
                b = t % 2
                dve.wait_ge(s_hi, (a * T + t + 1) * 3)
                low(k_lo[:, b, :], kv[:, b, 0:E], k_hi[:, b, :].bitcast(F32), ALU.max).then_inc(s_lo, 1)
                v = kv[:, b, E:2 * E].rearrange("p (h c) -> p h c", h=KE)
                for s in range(2):
                    at = pos_cols[:, bass.ds(pos, 1), t, s:s + 1].rearrange("p o s -> p (o s)")
                    low(v_lo[:, b, :, s, 0:P], v, v_hi[:, b, :, s, 0:P].bitcast(F32), ALU.mult, at
                        ).then_inc(s_lo, 1)

            def head_matrices(b):
                dve.wait_ge(s_accz, b + 1)
                for h in range(KE):
                    nc.vector.tensor_copy(kv_sum[:, h].rearrange("p s c -> p (s c)"), acc[h][:, 0:2 * VW]
                                          ).then_inc(s_sum, 1)
                dve.wait_ge(s_sum, (b + 1) * KE)
                for g in range(G):
                    r0, h = (g % 2) * GW, g // 2
                    src = slice(r0, r0 + GW)
                    num = slice(r0, r0 + GW)
                    dn = slice(GW - r0, 2 * GW - r0)
                    for s in range(2):
                        o0 = r0 if s == 0 else GW - r0
                        dst = slice(o0, o0 + GW)
                        nc.vector.tensor_tensor(kvt[dst, g, num], kv_sum[src, h, s, r0:r0 + GW], mask[src, :],
                                                ALU.mult).then_inc(s_kvt, 1)
                        nc.vector.tensor_scalar(kvt[dst, g, dn], mask[src, :], kv_sum[src, h, s, P:P + 1], None,
                                                ALU.mult).then_inc(s_kvt, 1)
                dve.wait_ge(s_kvt, (b + 1) * 4 * G)
                after(dve, s_atp, b * NB * G)
                nc.vector.tensor_copy(kvt_hi[:], kvt[:]).then_inc(s_kvh, 1)
                dve.wait_ge(s_kvh, b + 1)
                nc.vector.tensor_tensor(kvt_lo[:], kvt[:], kvt_hi[:].bitcast(F32), ALU.subtract).then_inc(s_kvl, 1)

            def q_cos(c, pos):
                dve.wait_ge(s_rows, c * 16 + 16)
                after(dve, s_ql, c * G)
                for g in range(G):
                    r0 = (g % 2) * GW
                    nc.vector.tensor_tensor(qsc[GW - r0:2 * GW - r0, g, :],
                                            q_all[r0:r0 + GW, g // 2, bass.ds(pos * CH, CH)],
                                            pos_rows[r0:r0 + GW, 1, :], ALU.mult).then_inc(s_qc, 1)

            def split_q(c):
                for g in range(G):
                    dve.wait_ge(s_qh, c * G + g + 1)
                    nc.vector.tensor_tensor(qsc_lo[:, g, :], qsc[:, g, :], qsc_hi[:, g, :].bitcast(F32),
                                            ALU.subtract).then_inc(s_ql, 1)

            def divide(c, k):
                for g in (2 * k, 2 * k + 1):
                    r0 = (g % 2) * GW
                    dve.wait_ge(s_atp, c * G + g + 1)
                    nc.vector.tensor_scalar(att[r0:r0 + GW, k, :], wp[g % 2][GW - r0:2 * GW - r0, :], EPS_DEN, None,
                                            ALU.max).then_inc(s_den, 1)
                dve.wait_ge(s_den, c * G + 2 * k + 2)
                nc.vector.reciprocal(att[:, k, :], att[:, k, :]).then_inc(s_rden, 1)
                dve.wait_ge(s_rden, c * KE + k + 1)
                for g in (2 * k, 2 * k + 1):
                    r0 = (g % 2) * GW
                    nc.vector.tensor_tensor(att[r0:r0 + GW, k, :], wp[g % 2][r0:r0 + GW, :], att[r0:r0 + GW, k, :],
                                            ALU.mult).then_inc(s_att, 1)

            def split_att(c, k):
                dve.wait_ge(s_ath, c * KE + k + 1)
                nc.vector.tensor_tensor(att_lo[:, k, :], att[:, k, :], att_hi[:, k, :].bitcast(F32),
                                        ALU.subtract).then_inc(s_atl, 1)

            def bias_o(c):
                after(dve, s_x2p, c * KE)
                for i in range(2):
                    dve.wait_ge(s_op, c * 2 + i + 1)
                    nc.vector.tensor_tensor(ob[:, 2 * i:2 * i + 2, :], wp[i][:].rearrange("p (t e) -> p t e", t=2),
                                            bo_row[:].rearrange("p (o e) -> p o e", o=1).to_broadcast([P, 2, E]), ALU.add).then_inc(s_ob, 1)
                dve.wait_ge(s_ob, c * 2 + 2)
                stats(ln_o, c, [ob[:, t, :] for t in range(T)])

            def stats_x1(c):
                dve.wait_ge(s_x1n, c + 1)
                stats(ln_2, c, [x1n[:, t, :] for t in range(T)])

            def split_x2(c):
                for h in range(KE):
                    dve.wait_ge(s_x2h, c * KE + h + 1)
                    nc.vector.tensor_tensor(x2_lo[:, h, :], wp[h][:], x2_hi[:, h, :], ALU.subtract
                                            ).then_inc(s_x2l, 1)

            def hidden(f, n):
                dve.wait_ge(s_hh, f * 2 * KF + n + 1)
                hi, lo = (h1_hi, h1_lo) if n < KF else (h2_hi, h2_lo)
                low(lo[:, n % KF, :], ffp[n % 2][:], hi[:, n % KF, :], ALU.max).then_inc(s_hl, 1)

            def layer0(f):
                for n in range(KF):
                    hidden(f, n)

            y_tiles = [yp[t // 2][:, (t % 2) * E:(t % 2 + 1) * E] for t in range(T)]

            def moments_y(f, i):
                dve.wait_ge(s_yp, f * T + 2 * i + 2)
                moments(ln_f, y_tiles, (2 * i, 2 * i + 1))

            def scale_shift_y(f):
                rstd(ln_f, f)
                nc.vector.tensor_scalar(ln_f.std[:], ln_f.rstd[:], ocs[:, 1:2], None, ALU.mult).then_inc(s_fc, 1)
                dve.wait_ge(s_fc, f + 1)
                shift(ln_f, f, ln_f.std[:])

            nc.vector.memset(zero_l[:].bitcast(U32), 0).then_inc(s_zero, 1)
            nc.vector.memset(eps_col[:], EPS_LN).then_inc(s_zero, 1)
            norm_x_stats(0)
            scale_shift(ln_a, 0)
            dve.wait_ge(s_first, 16 * FIRST_LOADS)
            nc.vector.tensor_copy(pos_hi[:], pos_cols[:]).then_inc(s_poshi, 1)
            dve.wait_ge(s_poshi, 1)
            nc.vector.tensor_tensor(pos_lo[:], pos_cols[:], pos_hi[:].bitcast(F32), ALU.subtract).then_inc(s_poslo, 1)
            for n, (lo, full, hi) in enumerate(((wkv_lo, wkv_f, wkv_hi), (wq_lo, wq_f, wq_hi))):
                dve.wait_ge(s_whi, n + 1)
                nc.vector.tensor_tensor(lo[:], full, hi[:].bitcast(F32), ALU.subtract).then_inc(s_wlo, 1)
            split_x(0)
            dve.wait_ge(s_whi, 3)
            nc.vector.tensor_tensor(wo_lo[:], wo_f, wo_hi[:].bitcast(F32), ALU.subtract).then_inc(s_wlo, 1)
            dve.wait_ge(s_late, 16 * LATE_LOADS)
            nc.vector.tensor_scalar(sgn[:], sv[:], 0.0, 2.0, ALU.is_ge, ALU.mult).then_inc(s_sc, 1)
            dve.wait_ge(s_sc, 1)
            nc.vector.tensor_scalar(sgn[:], sgn[:], -1.0, None, ALU.add).then_inc(s_sc, 1)
            dve.wait_ge(s_sc, 2)
            nc.vector.tensor_tensor(sab[:], sv[:], sgn[:], ALU.mult).then_inc(s_sc, 1)
            nc.vector.tensor_scalar(ksc[:, 0:1], sgn[:, 1:2], 2.0 * H1_SCALE, None, ALU.mult).then_inc(s_sc, 1)
            nc.vector.tensor_scalar(ksc[:, 1:2], sgn[:, 1:2], -H1_SCALE, None, ALU.mult).then_inc(s_sc, 1)
            dve.wait_ge(s_sc, 5)
            nc.vector.tensor_tensor(ocs[:, 0:1], sab[:, 0:1], sab[:, 1:2], ALU.mult).then_inc(s_sc, 1)
            dve.wait_ge(s_sc, 6)
            nc.vector.tensor_scalar(ocs[:, 1:2], ocs[:, 0:1], sv[:, 2:3], OUT_SCALE, ALU.mult, ALU.mult
                                    ).then_inc(s_sc, 1)
            dve.wait_ge(s_sc, 7)
            nc.vector.scalar_tensor_tensor(out=ocs[:, 2:3], in0=ocs[:, 1:2], scalar=1.0 / E, in1=ocs[:, 1:2],
                                           op0=ALU.mult, op1=ALU.mult).then_inc(s_sc, 1)
            dve.wait_ge(s_sc, 8)
            with dve.Fori(0, NB) as a:
                norm_x_stats(a + 1)
                bias_kv(a, 0, wide)
                scale_shift(ln_a, a + 1)
                bias_kv(a, 1, wide)
                split_kv(a, 0, a)
                bias_kv(a, 2, wide)
                split_kv(a, 1, a)
                bias_kv(a, 3, wide)
                split_kv(a, 2, a)
                split_kv(a, 3, a)
                split_x(a + 1)
            q_cos(0, 0)
            split_q(0)
            head_matrices(0)
            bias_kv(NB, 0, wide)
            bias_kv(NB, 1, wide)
            split_kv(NB, 0, 0)
            divide(0, 0)
            bias_kv(NB, 2, wide)
            split_kv(NB, 1, 0)
            divide(0, 1)
            split_att(0, 0)
            split_att(0, 1)
            bias_kv(NB, 3, wide)
            split_kv(NB, 2, 0)
            split_kv(NB, 3, 0)
            norm_x_stats(NB + 1)
            scale_shift(ln_a, NB + 1)
            bias_o(0)
            scale_shift(ln_o, 0)
            q_cos(1, 1)
            split_x(NB + 1)
            stats_x1(0)
            scale_shift(ln_2, 0)
            split_q(1)
            split_x2(0)
            layer0(0)

            def both(f, pos, pos_q, last):
                c, a = f + 1, f + (NB + 1)
                divide(c, 0)
                hidden(f, 8)
                bias_kv(a, 0, yp)
                bias_kv(a, 1, yp)
                split_kv(a, 0, pos)
                hidden(f, 9)
                split_kv(a, 1, pos)
                split_att(c, 0)
                divide(c, 1)
                bias_kv(a, 2, yp)
                hidden(f, 10)
                split_kv(a, 2, pos)
                split_att(c, 1)
                bias_kv(a, 3, yp)
                split_kv(a, 3, pos)
                hidden(f, 11)
                if not last:
                    norm_x_stats(a + 1)
                    scale_shift(ln_a, a + 1)
                bias_o(c)
                scale_shift(ln_o, c)
                hidden(f, 12)
                q_cos(c + 1, pos_q)
                hidden(f, 13)
                stats_x1(c)
                scale_shift(ln_2, c)
                hidden(f, 14)
                split_q(c + 1)
                hidden(f, 15)
                split_x2(c)
                moments_y(f, 0)
                if not last:
                    split_x(a + 1)
                hidden(f + 1, 0)
                moments_y(f, 1)
                for n in range(1, KF):
                    hidden(f + 1, n)
                variance(ln_f, f)
                scale_shift_y(f)

            def ff_at(f, pos_q):
                c = f + 1
                divide(c, 0)
                hidden(f, 8)
                hidden(f, 9)
                split_att(c, 0)
                divide(c, 1)
                hidden(f, 10)
                split_att(c, 1)
                hidden(f, 11)
                bias_o(c)
                scale_shift(ln_o, c)
                hidden(f, 12)
                if pos_q is not None:
                    q_cos(c + 1, pos_q)
                hidden(f, 13)
                stats_x1(c)
                scale_shift(ln_2, c)
                hidden(f, 14)
                if pos_q is not None:
                    split_q(c + 1)
                hidden(f, 15)
                split_x2(c)
                moments_y(f, 0)
                hidden(f + 1, 0)
                moments_y(f, 1)
                for n in range(1, KF):
                    hidden(f + 1, n)
                variance(ln_f, f)
                scale_shift_y(f)

            with dve.Fori(0, NB - 2) as f:
                both(f, f + 1, f + 2, False)
            both(NB - 2, NB - 1, 0, True)
            head_matrices(1)
            with dve.Fori(NB - 1, NCH - 2) as f:
                ff_at(f, f - (NB - 2))
            ff_at(NCH - 2, None)
            f = NCH - 1
            for n in range(KF, 2 * KF):
                hidden(f, n)
            moments_y(f, 0)
            moments_y(f, 1)
            variance(ln_f, f)
            scale_shift_y(f)

        @block.gpsimd
        def _(pool):
            def pos_in_v(a, pos, ts=range(T)):
                for t in ts:
                    b = t % 2
                    after(pool, s_acc, a * T if t < 2 else a * T + t - 1)
                    here = (slice(None), bass.ds(pos, 1), t, slice(None))
                    whole = pos_cols[here].to_broadcast([P, KE, 2])
                    for v, other in ((v_hi, pos_lo), (v_lo, pos_hi)):
                        part = other[:].bitcast(F32)[here].to_broadcast([P, KE, 2])
                        nc.gpsimd.tensor_tensor(v[:, b, :, :, P], whole, part, ALU.subtract).then_inc(s_pc, 1)

            def q_sin(c, pos, steps):
                if steps is not None:
                    pool.wait_ge(s_pc, steps * 2)
                pool.wait_ge(s_rows, c * 16 + 16)
                pool.wait_ge(s_q, c * KE + KE)
                after(pool, s_ql, c * G)
                for g in range(G):
                    r0 = (g % 2) * GW
                    nc.gpsimd.tensor_tensor(qsc[r0:r0 + GW, g, :], q_all[r0:r0 + GW, g // 2, bass.ds(pos * CH, CH)],
                                            pos_rows[r0:r0 + GW, 0, :], ALU.mult).then_inc(s_qs, 1)
                    pool.wait_ge(s_qs, c * G + g + 1)

            def add_x(c):
                pool.wait_ge(s_xr, c * 16 + 16)
                pool.wait_ge(s_on, c * T + T)
                nc.gpsimd.tensor_tensor(x1n[:], ob[:], x1n[:], ALU.add).then_inc(s_x1n, 1)

            def add_x1(f):
                pool.wait_ge(s_fo, f * T + 2 * T)
                pool.wait_ge(s_x1, f + 1)
                nc.gpsimd.tensor_tensor(fo[:], fo[:], x1[:], ALU.add).then_inc(s_out, 1)
                pool.wait_ge(s_out, f + 2)

            pool.wait_ge(s_poslo, 1)
            pool.sem_inc(s_out, 1)
            pos_in_v(0, 0)
            pool.wait_ge(s_sc, 5)
            nc.gpsimd.tensor_scalar(w0_half, k0_u8, sgn[:, 0:1], 0.0, ALU.mult, ALU.add).then_inc(s_w0h, 1)
            pool.wait_ge(s_w0h, 1)
            nc.gpsimd.tensor_tensor(w0[:], w0_half[:, 0:KE], w0_half[:, KE:2 * KE], ALU.subtract).then_inc(s_ffw, 1)
            nc.gpsimd.tensor_scalar(w1[:], k1_u8, ksc[:, 0:1], ksc[:, 1:2], ALU.mult, ALU.add).then_inc(s_ffw, 1)
            nc.gpsimd.tensor_scalar(w2[:], k2_u8, 2.0, -1.0, ALU.mult, ALU.add).then_inc(s_ffw, 1)
            with pool.Fori(1, NB) as a:
                pos_in_v(a, a)
            pool.wait_ge(s_wlo, 3)
            q_sin(0, 0, NB * T)
            pos_in_v(NB, 0)
            q_sin(1, 1, (NB + 1) * T)
            add_x(0)

            def both(f, pos_q):
                c, a = f + 1, f + (NB + 1)
                pos_in_v(a, c, (0, 1))
                q_sin(c + 1, pos_q, a * T + 2)
                pos_in_v(a, c, (2, 3))
                add_x(c)
                add_x1(f)

            with pool.Fori(0, NB - 2) as f:
                both(f, f + 2)
            both(NB - 2, 0)
            with pool.Fori(NB - 1, NCH - 2) as f:
                q_sin(f + 2, f - (NB - 2), None)
                add_x(f + 1)
                add_x1(f)
            add_x(NCH - 1)
            add_x1(NCH - 2)
            add_x1(NCH - 1)


def kernel(L0_attn_x, L0_attn_Wq, L0_attn_bq, L0_attn_Wk, L0_attn_bk, L0_attn_Wv, L0_attn_bv, L0_attn_Wo,
           L0_attn_bo, L0_ffn_k0, L0_ffn_k1, L0_ffn_k2, L0_ffn_s0, L0_ffn_s1, L0_ffn_s2):
    import concourse.bacc as bacc
    from concourse.bass_utils import run_bass_kernel_spmd

    def a(v):
        return np.asarray(v)

    def rows(*v):
        return np.ascontiguousarray(np.concatenate([a(u).reshape(1, -1) for u in v], axis=1))

    pos_rows, pos_cols, ident, mask = shape_tables()
    arrays = {
        "x": np.ascontiguousarray(a(L0_attn_x).reshape(B * L, E)),
        "wq_t": np.ascontiguousarray(a(L0_attn_Wq).T),
        "wkv_t": np.ascontiguousarray(np.concatenate([a(L0_attn_Wk).T, a(L0_attn_Wv).T], axis=1)),
        "wo_t": np.ascontiguousarray(a(L0_attn_Wo).T),
        "bq": a(L0_attn_bq),
        "bkv": rows(L0_attn_bk, L0_attn_bv),
        "bo": rows(L0_attn_bo),
        "k0": np.ascontiguousarray(a(L0_ffn_k0)).view(np.uint32),
        "k1": np.ascontiguousarray(a(L0_ffn_k1)).view(np.uint32),
        "k2": np.ascontiguousarray(a(L0_ffn_k2)).view(np.uint32),
        "s0": a(L0_ffn_s0).reshape(1, 1),
        "s1": a(L0_ffn_s1).reshape(1, 1),
        "s2": a(L0_ffn_s2).reshape(1, 1),
        "pos_rows_in": pos_rows, "pos_cols_in": pos_cols, "ident_in": ident, "mask_in": mask,
    }
    nc = bacc.Bacc("TRN2", target_bir_lowering=False, num_devices=1)
    d = {n: nc.dram_tensor(n, list(v.shape), mybir.dt.from_np(v.dtype), kind="ExternalInput").ap()
         for n, v in arrays.items()}
    out = nc.dram_tensor("out", [B * L, E], F32, kind="ExternalOutput").ap()
    build(nc, d["x"], d["wq_t"], d["wkv_t"], d["wo_t"], d["bq"], d["bkv"], d["bo"], d["k0"], d["k1"], d["k2"],
          (d["s0"], d["s1"], d["s2"]), d["pos_rows_in"], d["pos_cols_in"], d["ident_in"], d["mask_in"], out)
    r = run_bass_kernel_spmd(nc, [arrays], core_ids=[0])
    return r.results[0]["out"].reshape(B, L, E)
```

```python
from contextlib import ExitStack

import numpy as np

import concourse.bass as bass
from concourse import mybir

F32 = mybir.dt.float32
F32R = mybir.dt.float32r
F16 = mybir.dt.float16
U8 = mybir.dt.uint8
U32 = mybir.dt.uint32
ALU = mybir.AluOpType
ACT = mybir.ActivationFunctionType

P = 128
B, L, E = 2, 4096, 256
HEADS = 16
HD = E // HEADS
F = 1024
T = 4
CH = T * P
NB = L // CH
NCH = B * NB
KE = E // P
KF = F // P
G = 4
GW = E // G
VW = P + 1
EPS_DEN = 1e-4
EPS_LN = 1e-5
H1_SCALE = 2.0 ** -4
OUT_SCALE = 8.0 / H1_SCALE


def shape_tables():
    idx = (np.float32(np.pi / 2) * np.arange(1, L + 1, dtype=np.float32) / np.float32(L)).astype(np.float32)
    sc = np.stack([np.sin(idx), np.cos(idx)]).astype(np.float32)
    by = sc.reshape(2, NB, P, T)
    rows = np.tile(by.transpose(1, 0, 3, 2).reshape(NB, 2 * CH), (B, 1))
    cols = np.ascontiguousarray(by.transpose(2, 1, 3, 0)).reshape(P, NB * T * 2)
    ident = np.eye(P, dtype=np.float32)
    r, c = np.arange(P)[:, None] % GW, np.arange(GW)[None, :]
    mask = (r // HD == c // HD).astype(np.float32)
    return rows, cols, ident, mask


def build(nc, x, wq_t, wkv_t, wo_t, bq, bkv, bo, k0, k1, k2, scales, rows_d, cols_d, ident_d, mask_d, out):
    ctx = ExitStack()
    with ctx:
        def sb(name, shape, dt=F32):
            return ctx.enter_context(nc.sbuf_tensor(name, shape, dt))

        def sem(name):
            return ctx.enter_context(nc.semaphore(name))

        ident = sb("ident", [P, P])
        mask = sb("mask", [P, GW])
        pos_cols = sb("pos_cols", [P, NB, T, 2])
        pos_hi = sb("pos_hi", [P, NB, T, 2], F32R)
        pos_lo = sb("pos_lo", [P, NB, T, 2], F32R)
        wq_hi = sb("wq_hi", [P, KE, E], F32R)
        wq_lo = sb("wq_lo", [P, KE, E], F32R)
        wkv_hi = sb("wkv_hi", [P, KE, 2 * E], F32R)
        wkv_lo = sb("wkv_lo", [P, KE, 2 * E], F32R)
        wo_hi = sb("wo_hi", [P, KE, E], F32R)
        wo_lo = sb("wo_lo", [P, KE, E], F32R)
        bq_col = sb("bq_col", [P, KE])
        bkv_row = sb("bkv_row", [P, 2 * E])
        bo_row = sb("bo_row", [P, E])
        w0 = sb("w0", [P, KE, F], F16)
        w1 = sb("w1", [P, KF, F], F16)
        w2 = sb("w2", [P, KF, E], F16)
        sv = sb("sv", [P, 3])
        sgn = sb("sgn", [P, 3])
        sab = sb("sab", [P, 3])
        ksc = sb("ksc", [P, 4])
        ocs = sb("ocs", [P, 3])

        xa = sb("xa", [P, T, E])
        xn = sb("xn", [P, T, E])
        xt_hi = sb("xt_hi", [P, KE, CH], F32R)
        xt_lo = sb("xt_lo", [P, KE, CH], F32R)
        q_all = sb("q_all", [P, KE, L])
        kv = sb("kv", [P, 2, 2 * E])
        k_hi = sb("k_hi", [P, 2, E], F32R)
        k_lo = sb("k_lo", [P, 2, E], F32R)
        v_hi = sb("v_hi", [P, 2, KE, 2, VW], F32R)
        v_lo = sb("v_lo", [P, 2, KE, 2, VW], F32R)
        eps_col = sb("eps_col", [P, 1])
        table = sb("table", [P, 1])
        zero_l = sb("zero_l", [P, P], F32R)
        kvt_hi = sb("kvt_hi", [P, G, P], F32R)
        kvt_lo = sb("kvt_lo", [P, G, P], F32R)

        pos_rows = sb("pos_rows", [P, 2, CH])
        qsc = sb("qsc", [P, G, CH])
        qsc_hi = sb("qsc_hi", [P, G, CH], F32R)
        qsc_lo = sb("qsc_lo", [P, G, CH], F32R)
        att = sb("att", [P, KE, CH])
        att_hi = sb("att_hi", [P, KE, CH], F32R)
        att_lo = sb("att_lo", [P, KE, CH], F32R)
        x1n = sb("x1n", [P, T, E])
        ob = sb("ob", [P, T, E])
        x1 = sb("x1", [P, T, E])
        kv_sum = ob[:].rearrange("p t e -> p (t e)")[:, 0:KE * 2 * VW].rearrange("p (h s c) -> p h s c", h=KE, s=2)
        kvt = att[:, 0, :].rearrange("p (g m) -> p g m", g=G)
        x2_hi = sb("x2_hi", [P, KE, CH], F16)
        x2_lo = sb("x2_lo", [P, KE, CH], F16)
        h1_hi = sb("h1_hi", [P, KF, CH], F16)
        h1_lo = sb("h1_lo", [P, KF, CH], F16)
        h2_hi = sb("h2_hi", [P, KF, CH], F16)
        h2_lo = sb("h2_lo", [P, KF, CH], F16)
        fo = sb("fo", [P, T, E])

        wq_f = qsc[:, 0, :].rearrange("p (k e) -> p k e", k=KE)
        wo_f = qsc[:, 1, :].rearrange("p (k e) -> p k e", k=KE)
        wkv_f = qsc[:, 2:4, :]
        k1_u8 = h1_hi[:].bitcast(U8).rearrange("p k c -> p (k c)").rearrange("p (k f) -> p k f", k=KF)
        k0_u8 = h1_lo[:].bitcast(U8).rearrange("p k c -> p (k c)")[:, 0:4 * F].rearrange("p (k f) -> p k f", k=4)
        k2_u8 = h1_lo[:].bitcast(U8).rearrange("p k c -> p (k c)")[:, 4 * F:4 * F + KF * E].rearrange(
            "p (k f) -> p k f", k=KF)
        w0_half = h2_hi[:].rearrange("p k c -> p (k c)").rearrange("p (k f) -> p k f", k=4)

        class Norm:

            def __init__(self, name):
                self.stats = sb(name + "_stats", [P, T, 6])
                self.d = sb(name + "_d", [P, 4, T])
                self.var = sb(name + "_var", [P, T])
                self.std = sb(name + "_std", [P, T])
                self.rstd = sb(name + "_rstd", [P, T])
                self.nmr = sb(name + "_nmr", [P, T])
                self.s_stats = sem(name + "_stats_done")
                self.s_d = sem(name + "_d_done")
                self.s_d2 = sem(name + "_d2_done")
                self.s_var = sem(name + "_var_done")
                self.s_std = sem(name + "_std_done")
                self.s_rstd = sem(name + "_rstd_done")
                self.s_nmr = sem(name + "_nmr_done")

        ln_a, ln_o, ln_2, ln_f = Norm("ln_a"), Norm("ln_o"), Norm("ln_2"), Norm("ln_f")

        def bank(name):
            return ctx.enter_context(nc.psum_tensor(name, [P, 512], F32))

        acc = [bank("acc0"), bank("acc1")]
        ffp = [bank("ffp0"), bank("ffp1")]
        yp = [bank("yp0"), bank("yp1")]
        wp = [bank("wp0"), bank("wp1")]

        wide = [ffp[0], ffp[1], yp[0], yp[1]]

        def hidden_bank(n):
            return [ffp[0], ffp[1], wp[0], wp[1]][n % 4] if n < KF else ffp[n % 2]

        s_ident = sem("ident_loaded")
        s_wkvf = sem("wkv_loaded")
        s_first = sem("first_loads")
        s_scales = sem("scales_loaded")
        s_late = sem("late_loads")
        s_xa = sem("xa_loaded")
        s_xr = sem("xr_loaded")
        s_rows = sem("pos_rows_loaded")
        s_free = sem("fo_free")
        s_whi = sem("w_hi_ready")
        s_wlo = sem("w_lo_ready")
        s_zero = sem("zero_ready")
        s_poshi = sem("pos_hi_ready")
        s_poslo = sem("pos_lo_ready")
        s_sc = sem("scale_terms")
        s_w0h = sem("w0_halves")
        s_ffw = sem("ffn_weights_ready")

        s_xn = sem("xn_ready")
        s_xtp = sem("xt_in_psum")
        s_xth = sem("xt_hi_ready")
        s_xtl = sem("xt_lo_ready")
        s_qp = sem("q_in_psum")
        s_q = sem("q_kept")
        s_kvp = sem("kv_in_psum")
        s_kv = sem("kv_biased")
        s_hi = sem("kv_hi_ready")
        s_lo = sem("kv_lo_ready")
        s_pc = sem("pos_in_v")
        s_acc = sem("acc_step_done")
        s_accz = sem("acc_closed")
        s_sum = sem("kv_sum_ready")
        s_kvt = sem("kvt_ready")
        s_kvh = sem("kvt_hi_ready")
        s_kvl = sem("kvt_lo_ready")

        s_qs = sem("q_sin_ready")
        s_qc = sem("q_cos_ready")
        s_qh = sem("qsc_hi_ready")
        s_ql = sem("qsc_lo_ready")
        s_atp = sem("att_in_psum")
        s_den = sem("den_ready")
        s_rden = sem("rden_ready")
        s_att = sem("att_ready")
        s_ath = sem("att_hi_ready")
        s_atl = sem("att_lo_ready")
        s_op = sem("o_in_psum")
        s_ob = sem("o_biased")
        s_on = sem("o_normed")
        s_x1n = sem("x1n_ready")
        s_x1 = sem("x1_kept")
        s_xn2 = sem("xn2_ready")
        s_x2p = sem("x2_in_psum")
        s_x2h = sem("x2_hi_ready")
        s_x2l = sem("x2_lo_ready")

        s_hp = sem("h_in_psum")
        s_hh = sem("h_hi_ready")
        s_hl = sem("h_lo_ready")
        s_yp = sem("y_in_psum")
        s_fc = sem("f_scale_ready")
        s_fo = sem("f_normed")
        s_out = sem("out_ready")

        x_c = x.rearrange("(c p t) e -> c p (t e)", p=P, t=T)
        out_c = out.rearrange("(c p t) e -> c p (t e)", p=P, t=T)

        def after(eng, s, count):
            if not isinstance(count, int) or count > 0:
                eng.wait_ge(s, count)

        def pick(ap, i):
            return ap[bass.ds(i, 1)].rearrange("o p f -> (o p) f")

        FIRST_LOADS, SCALE_LOADS, LATE_LOADS = 6, 4, 5
        block = ctx.enter_context(nc.Block())

        @block.sync
        def _(sp):
            def load_x(a):
                src = pick(x_c, a)
                sp.wait_ge(s_xn, a * T)
                sp.dma_start(xa[:].rearrange("p t e -> p (t e)"), src).then_inc(s_xa, 16)

            def load_rows(c):
                src = rows_d[bass.ds(c, 1), :].to_broadcast([P, 2 * CH])
                after(sp, s_qs, c * G)
                after(sp, s_qc, c * G)
                sp.dma_start(pos_rows[:].rearrange("p s c -> p (s c)"), src).then_inc(s_rows, 16)

            def load_xr(c):
                src = pick(x_c, c)
                after(sp, s_x1, c)
                sp.dma_start(x1n[:].rearrange("p t e -> p (t e)"), src).then_inc(s_xr, 16)

            def store(f):
                dst = pick(out_c, f)
                sp.wait_ge(s_out, f + 2)
                sp.dma_start(dst, fo[:].rearrange("p t e -> p (t e)")).then_inc(s_free, 16)

            sp.dma_start(xa[:].rearrange("p t e -> p (t e)"), x_c[0]).then_inc(s_xa, 16)
            sp.dma_start(ident[:], ident_d).then_inc(s_ident, 16)
            sp.dma_start(wkv_f, wkv_t.rearrange("(k p) f -> p k f", p=P)).then_inc(s_wkvf, 16)
            sp.dma_start(wq_f, wq_t.rearrange("(k p) f -> p k f", p=P)).then_inc(s_first, 16)
            sp.dma_start(bkv_row[:], bkv.to_broadcast([P, 2 * E])).then_inc(s_first, 16)
            sp.dma_start(bq_col[:], bq.rearrange("(k p) -> p k", p=P), allow_slow_non_contiguous=True).then_inc(s_first, 16)
            sp.dma_start(pos_cols[:].rearrange("p c t s -> p (c t s)"), cols_d).then_inc(s_first, 16)
            sp.dma_start(wo_f, wo_t.rearrange("(k p) f -> p k f", p=P)).then_inc(s_first, 16)
            sp.dma_start(bo_row[:], bo.to_broadcast([P, E])).then_inc(s_first, 16)
            sp.dma_start(mask[:], mask_d).then_inc(s_scales, 16)
            for n in range(3):
                sp.dma_start(sv[:, n:n + 1], scales[n].to_broadcast([P, 1]),
                             allow_slow_non_contiguous=True).then_inc(s_scales, 16)
            load_x(1)
            sp.dma_start(k0_u8.bitcast(U32), k0.rearrange("(k p) f -> p k f", p=P)).then_inc(s_late, 16)
            half = KF // 2
            sp.dma_start(k1_u8[:, 0:half].bitcast(U32), k1[0:half * P].rearrange("(k p) f -> p k f", p=P)).then_inc(s_late, 16)
            sp.dma_start(k1_u8[:, half:KF].bitcast(U32), k1[half * P:F].rearrange("(k p) f -> p k f", p=P)).then_inc(s_late, 16)
            sp.dma_start(k2_u8[:, 0:half].bitcast(U32), k2[0:half * P].rearrange("(k p) f -> p k f", p=P)).then_inc(s_late, 16)
            sp.dma_start(k2_u8[:, half:KF].bitcast(U32), k2[half * P:F].rearrange("(k p) f -> p k f", p=P)).then_inc(s_late, 16)
            load_x(2)
            load_rows(0)
            load_xr(0)
            with sp.Fori(3, NB + 1) as a:
                load_x(a)
            load_rows(1)
            load_x(NB + 1)
            load_x(NB + 2)
            load_rows(2)
            load_xr(1)
            load_rows(3)
            load_x(NB + 3)
            store(0)
            with sp.Fori(1, NB - 3) as f:
                load_x(f + (NB + 3))
                load_rows(f + 3)
                load_xr(f + 1)
                store(f)
            with sp.Fori(NB - 3, NCH - 3) as f:
                load_rows(f + 3)
                load_xr(f + 1)
                store(f)
            for f in (NCH - 3, NCH - 2):
                load_xr(f + 1)
                store(f)
            store(NCH - 1)
            sp.wait_ge(s_free, 16 * (NCH + 1))

        @block.tensor
        def _(pe):
            def mm(dst, lhs, rhs, start, stop):
                return nc.tensor.matmul(dst, lhs, rhs, start=start, stop=stop)

            def passes(dst, pairs, acc_open=False):
                last = None
                n = 0
                for (lh, ll), (rh, rl) in pairs:
                    for u, v in ((lh, rh), (lh, rl), (ll, rh)):
                        last = mm(dst, u, v, n == 0 and not acc_open, n == 3 * len(pairs) - 1 and not acc_open)
                        n += 1
                return last

            def transpose_x(a, banks=wp):
                pe.wait_ge(s_xn, a * T + T)
                for h in range(KE):
                    for t in range(T):
                        last = nc.tensor.transpose(banks[h][:, t * P:(t + 1) * P], xn[:, t, h * P:(h + 1) * P], ident[:])
                    last.then_inc(s_xtp, 1)

            def project_q(a):
                pe.wait_ge(s_xtl, a * KE + KE)
                for h in range(KE):
                    m = slice(h * P, (h + 1) * P)
                    passes(wp[h][:], [((wq_hi[:, k, m], wq_lo[:, k, m]), (xt_hi[:, k, :], xt_lo[:, k, :]))
                                      for k in range(KE)]).then_inc(s_qp, 1)

            def project_kv(a, t, banks):
                if t >= len(banks):
                    pe.wait_ge(s_kv, a * T + t - len(banks) + 1)
                m = slice(t * P, (t + 1) * P)
                passes(banks[t % len(banks)][:], [((xt_hi[:, k, m], xt_lo[:, k, m]), (wkv_hi[:, k, :], wkv_lo[:, k, :]))
                                      for k in range(KE)]).then_inc(s_kvp, 1)

            def sum_kv(a, t):
                pe.wait_ge(s_lo, (a * T + t + 1) * 3)
                pe.wait_ge(s_pc, (a * T + t + 1) * 2)
                b = t % 2
                for h in range(KE):
                    m = slice(h * P, (h + 1) * P)
                    last = passes(acc[h][:, 0:2 * VW], [((k_hi[:, b, m], k_lo[:, b, m]),
                                  (v_hi[:, b, h].rearrange("p s c -> p (s c)"),
                                   v_lo[:, b, h].rearrange("p s c -> p (s c)")))], acc_open=True)
                last.then_inc(s_acc, 1)

            def idle_products(n):
                for _ in range(n):
                    mm(acc[0][:, 0:P], zero_l[:], zero_l[:], True, True)

            def open_acc():
                for h in range(KE):
                    mm(acc[h][:, 0:2 * VW], zero_l[:], wkv_hi[:, 0, 0:2 * VW], True, False)

            def close_acc():
                for h in range(KE):
                    last = mm(acc[h][:, 0:2 * VW], zero_l[:], wkv_hi[:, 0, 0:2 * VW], False, True)
                last.then_inc(s_accz, 1)

            def attend(c, g):
                pe.wait_ge(s_ql, c * G + g + 1)
                if g >= 2:
                    pe.wait_ge(s_att, c * G + g - 1)
                passes(yp[g % 2][:], [((kvt_hi[:, g, :], kvt_lo[:, g, :]), (qsc_hi[:, g, :], qsc_lo[:, g, :]))]
                       ).then_inc(s_atp, 1)

            def project_o(c):
                pe.wait_ge(s_atl, c * KE + KE)
                for t in range(T):
                    m = slice(t * P, (t + 1) * P)
                    last = passes(wp[t // 2][:, (t % 2) * E:(t % 2 + 1) * E],
                                  [((att_hi[:, k, m], att_lo[:, k, m]), (wo_hi[:, k, :], wo_lo[:, k, :]))
                                   for k in range(KE)])
                    if t % 2:
                        last.then_inc(s_op, 1)

            def transpose_x2(c):
                pe.wait_ge(s_xn2, c * T + T)
                for h in range(KE):
                    for t in range(T):
                        last = nc.tensor.transpose(wp[h][:, t * P:(t + 1) * P], ob[:, t, h * P:(h + 1) * P], ident[:])
                    last.then_inc(s_x2p, 1)

            def hidden(f, n, w, hi, lo, kn):
                j = n % KF
                if 4 <= n < KF + 2:
                    pe.wait_ge(s_hl, f * 2 * KF + n - 3)
                elif n >= KF + 2:
                    pe.wait_ge(s_hl, f * 2 * KF + n - 1)
                dst = hidden_bank(n)[:]
                m = slice(j * P, (j + 1) * P)
                for k in range(kn):
                    if n == KF and k >= 4:
                        pe.wait_ge(s_hl, f * 2 * KF + k + 1)
                    mm(dst, w[:, k, m], hi[:, k, :], k == 0, False)
                    last = mm(dst, w[:, k, m], lo[:, k, :], False, k == kn - 1)
                last.then_inc(s_hp, 1)

            def layer0(f):
                pe.wait_ge(s_x2l, f * KE + KE)
                for j in range(KF):
                    hidden(f, j, w0, x2_hi, x2_lo, KE)

            def layer1(f, j):
                hidden(f, KF + j, w1, h1_hi, h1_lo, KF)

            def layer2(f, t):
                if t == 0:
                    pe.wait_ge(s_hl, (f + 1) * 2 * KF - 1)
                m = slice(t * P, (t + 1) * P)
                dst = yp[t // 2][:, (t % 2) * E:(t % 2 + 1) * E]
                for k in range(KF):
                    if t == 0 and k == KF - 1:
                        pe.wait_ge(s_hl, (f + 1) * 2 * KF)
                    mm(dst, h2_hi[:, k, m], w2[:, k, :], k == 0, False)
                    last = mm(dst, h2_lo[:, k, m], w2[:, k, :], False, k == KF - 1)
                last.then_inc(s_yp, 1)

            pe.wait_ge(s_zero, 1)
            with pe.Fori(0, 9):
                idle_products(4)
            pe.wait_ge(s_ident, 16)
            transpose_x(0)
            idle_products(5)
            pe.wait_ge(s_wlo, 1)
            open_acc()

            with pe.Fori(0, NB) as a:
                pe.wait_ge(s_xtl, a * KE + KE)
                project_kv(a, 0, wide)
                project_kv(a, 1, wide)
                pe.wait_ge(s_wlo, 2)
                project_q(a)
                project_kv(a, 2, wide)
                sum_kv(a, 0)
                project_kv(a, 3, wide)
                sum_kv(a, 1)
                pe.wait_ge(s_q, a * KE + KE)
                transpose_x(a + 1)
                sum_kv(a, 2)
                sum_kv(a, 3)

            close_acc()
            pe.wait_ge(s_xtl, (NB + 1) * KE)
            project_kv(NB, 0, ffp)
            project_kv(NB, 1, ffp)
            pe.wait_ge(s_kvl, 1)
            attend(0, 0)
            attend(0, 1)
            attend(0, 2)
            attend(0, 3)
            project_kv(NB, 2, ffp)
            project_q(NB)
            pe.wait_ge(s_sum, KE)
            open_acc()
            sum_kv(NB, 0)
            project_kv(NB, 3, ffp)
            pe.wait_ge(s_att, G)
            transpose_x(NB + 1, yp)
            pe.wait_ge(s_q, (NB + 1) * KE)
            project_o(0)
            pe.wait_ge(s_xtl, (NB + 2) * KE)
            attend(1, 0)
            attend(1, 1)
            pe.wait_ge(s_ob, KE)
            transpose_x2(0)
            sum_kv(NB, 1)
            attend(1, 2)
            attend(1, 3)
            pe.wait_ge(s_kv, NB * T + 3)
            pe.wait_ge(s_ffw, 4)
            pe.wait_ge(s_x2l, KE)
            hidden(0, 0, w0, x2_hi, x2_lo, KE)
            pe.wait_ge(s_kv, (NB + 1) * T)
            for n in range(1, 8):
                hidden(0, n, w0, x2_hi, x2_lo, KE)
            layer1(0, 0)
            sum_kv(NB, 2)
            project_kv(NB + 1, 0, wp)
            project_kv(NB + 1, 1, wp)
            layer1(0, 1)
            sum_kv(NB, 3)
            project_kv(NB + 1, 2, wp)
            project_kv(NB + 1, 3, wp)
            layer1(0, 2)
            sum_kv(NB + 1, 0)
            pe.wait_ge(s_kv, (NB + 2) * T)
            project_q(NB + 1)
            layer1(0, 3)
            pe.wait_ge(s_q, (NB + 2) * KE)
            project_o(1)
            sum_kv(NB + 1, 1)
            attend(2, 0)
            attend(2, 1)
            layer1(0, 4)
            layer1(0, 5)
            pe.wait_ge(s_ob, 2 * KE)
            transpose_x(NB + 2)
            layer1(0, 6)
            pe.wait_ge(s_xtl, (NB + 3) * KE)
            project_kv(NB + 2, 0, wp)
            attend(2, 2)
            attend(2, 3)
            project_kv(NB + 2, 1, wp)
            sum_kv(NB + 1, 2)
            layer1(0, 7)
            project_kv(NB + 2, 2, wp)
            sum_kv(NB + 1, 3)
            sum_kv(NB + 2, 0)
            project_kv(NB + 2, 3, wp)
            pe.wait_ge(s_att, 3 * G)
            layer2(0, 0)
            pe.wait_ge(s_kv, (NB + 3) * T)
            transpose_x2(1)
            sum_kv(NB + 2, 1)
            sum_kv(NB + 2, 2)
            layer2(0, 1)
            pe.wait_ge(s_hl, 2 * KF - 1)
            pe.wait_ge(s_x2l, 2 * KE)
            hidden(1, 0, w0, x2_hi, x2_lo, KE)
            project_q(NB + 2)
            layer2(0, 2)
            pe.wait_ge(s_q, (NB + 3) * KE)
            transpose_x(NB + 3)
            layer2(0, 3)
            pe.wait_ge(s_hl, 2 * KF)
            hidden(1, 1, w0, x2_hi, x2_lo, KE)
            pe.wait_ge(s_xtl, (NB + 4) * KE)
            for n in range(2, 8):
                hidden(1, n, w0, x2_hi, x2_lo, KE)
            sum_kv(NB + 2, 3)

            def both(f, last):
                c, a = f + 1, f + (NB + 2)
                layer1(f, 0)
                project_o(c)
                layer1(f, 1)
                pe.wait_ge(s_fo, f * T + T)
                attend(c + 1, 0)
                attend(c + 1, 1)
                pe.wait_ge(s_ob, c * 2 + 2)
                project_kv(a, 0, wp)
                project_kv(a, 1, wp)
                layer1(f, 2)
                layer1(f, 3)
                attend(c + 1, 2)
                attend(c + 1, 3)
                sum_kv(a, 0)
                project_kv(a, 2, wp)
                layer1(f, 4)
                sum_kv(a, 1)
                project_kv(a, 3, wp)
                layer1(f, 5)
                sum_kv(a, 2)
                pe.wait_ge(s_kv, a * T + T)
                transpose_x2(c)
                layer1(f, 6)
                sum_kv(a, 3)
                if last:
                    close_acc()
                pe.wait_ge(s_x2l, c * KE + KE)
                project_q(a)
                layer1(f, 7)
                pe.wait_ge(s_att, c * G + 2 * G)
                layer2(f, 0)
                layer2(f, 1)
                if not last:
                    pe.wait_ge(s_q, a * KE + KE)
                    transpose_x(a + 1)
                layer2(f, 2)
                layer2(f, 3)
                if last:
                    pe.wait_ge(s_q, a * KE + KE)
                else:
                    pe.wait_ge(s_xtl, a * KE + 2 * KE)
                layer0(f + 1)

            def ff_at(f, attention=True):
                c = f + 1
                layer1(f, 0)
                project_o(c)
                layer1(f, 1)
                pe.wait_ge(s_fo, f * T + T)
                if attention:
                    attend(c + 1, 0)
                    attend(c + 1, 1)
                layer1(f, 2)
                layer1(f, 3)
                if attention:
                    attend(c + 1, 2)
                    attend(c + 1, 3)
                layer1(f, 4)
                layer1(f, 5)
                transpose_x2(c)
                layer1(f, 6)
                layer1(f, 7)
                if attention:
                    pe.wait_ge(s_att, c * G + 2 * G)
                for t in range(T):
                    layer2(f, t)
                layer0(f + 1)

            with pe.Fori(1, NB - 3) as f:
                both(f, False)
            both(NB - 3, True)
            pe.wait_ge(s_kvl, 2)
            with pe.Fori(NB - 2, NCH - 2) as f:
                ff_at(f)
            ff_at(NCH - 2, False)
            f = NCH - 1
            for j in range(KF):
                layer1(f, j)
            pe.wait_ge(s_fo, f * T + T)
            for t in range(T):
                layer2(f, t)

        @block.scalar
        def _(act):
            def std(ln, n, scale=1.0 / E):
                act.wait_ge(ln.s_var, n + 1)
                nc.scalar.activation(ln.std[:], ln.var[:], ACT.Sqrt, bias=eps_col[:], scale=scale
                                     ).then_inc(ln.s_std, 1)

            def norm(ln, n, dst, src, done):
                act.wait_ge(ln.s_nmr, n + 1)
                for t in range(T):
                    nc.scalar.activation(dst[:, t, :], src[:, t, :], ACT.Identity, bias=ln.nmr[:, t:t + 1],
                                         scale=ln.rstd[:, t:t + 1]).then_inc(done, 1)

            def norm_x(a):
                after(act, s_xtp, a * KE)
                norm(ln_a, a, xn, xa, s_xn)

            def split_x(a, banks=wp):
                for h in range(KE):
                    act.wait_ge(s_xtp, a * KE + h + 1)
                    nc.scalar.activation(xt_hi[:, h, :], banks[h][:], ACT.Copy).then_inc(s_xth, 1)

            def keep_q(a, pos):
                for h in range(KE):
                    act.wait_ge(s_qp, a * KE + h + 1)
                    nc.scalar.activation(q_all[:, h, bass.ds(pos * CH, CH)], wp[h][:], ACT.Relu,
                                         bias=bq_col[:, h:h + 1]).then_inc(s_q, 1)

            def split_kv(a, t, pos):
                b = t % 2
                act.wait_ge(s_kv, a * T + t + 1)
                if t >= 2:
                    act.wait_ge(s_acc, a * T + t - 1)
                nc.scalar.activation(k_hi[:, b, :], kv[:, b, 0:E], ACT.Relu).then_inc(s_hi, 1)
                v = kv[:, b, E:2 * E].rearrange("p (h c) -> p h c", h=KE)
                for s in range(2):
                    at = pos_cols[:, bass.ds(pos, 1), t, s:s + 1].rearrange("p o s -> p (o s)")
                    nc.scalar.activation(v_hi[:, b, :, s, 0:P], v, ACT.Copy, scale=at).then_inc(s_hi, 1)

            def split_q(c):
                for g in range(G):
                    act.wait_ge(s_qs, c * G + g + 1)
                    act.wait_ge(s_qc, c * G + g + 1)
                    if g == 0:
                        after(act, s_atp, c * G)
                    nc.scalar.activation(qsc_hi[:, g, :], qsc[:, g, :], ACT.Copy).then_inc(s_qh, 1)

            def split_att(c, k):
                act.wait_ge(s_att, c * G + 2 * k + 2)
                after(act, s_op, c * 2)
                nc.scalar.activation(att_hi[:, k, :], att[:, k, :], ACT.Copy).then_inc(s_ath, 1)

            def split_x2(c):
                for h in range(KE):
                    act.wait_ge(s_x2p, c * KE + h + 1)
                    nc.scalar.activation(x2_hi[:, h, :], wp[h][:], ACT.Copy).then_inc(s_x2h, 1)

            def hidden(f, n):
                act.wait_ge(s_hp, f * 2 * KF + n + 1)
                dst = (h1_hi if n < KF else h2_hi)[:, n % KF, :]
                nc.scalar.activation(dst, hidden_bank(n)[:], ACT.Relu).then_inc(s_hh, 1)

            def keep_x1(f):
                act.wait_ge(s_x1n, f * T + T)
                act.wait_ge(s_out, f + 1)
                nc.scalar.copy(x1[:], x1n[:]).then_inc(s_x1, 1)

            def norm_y(f):
                act.wait_ge(ln_f.s_nmr, f + 1)
                act.wait_ge(s_free, f * 16 + 16)
                for t in range(T):
                    nc.scalar.activation(fo[:, t, :], yp[t // 2][:, (t % 2) * E:(t % 2 + 1) * E], ACT.Identity,
                                         bias=ln_f.nmr[:, t:t + 1], scale=ln_f.std[:, t:t + 1]).then_inc(s_fo, 1)

            def ff_end(f):
                for n in range(KF):
                    if n == 4:
                        std(ln_f, f, ocs[:, 2:3])
                    hidden(f + 1, n)
                norm_y(f)

            act.sem_inc(s_free, 16)
            act.sem_inc(s_fo, T)
            act.wait_ge(s_zero, 2)
            nc.scalar.activation(table[:], eps_col[:], ACT.Sqrt)
            std(ln_a, 0)
            norm_x(0)
            act.wait_ge(s_wkvf, 16)
            nc.scalar.activation(wkv_hi[:], wkv_f, ACT.Copy).then_inc(s_whi, 1)
            split_x(0)
            act.wait_ge(s_first, 16 * FIRST_LOADS)
            nc.scalar.activation(wq_hi[:], wq_f, ACT.Copy).then_inc(s_whi, 1)
            nc.scalar.activation(wo_hi[:], wo_f, ACT.Copy).then_inc(s_whi, 1)

            def project(a):
                std(ln_a, a + 1)
                split_kv(a, 0, a)
                split_kv(a, 1, a)
                keep_q(a, a)
                norm_x(a + 1)
                split_kv(a, 2, a)
                split_kv(a, 3, a)
                split_x(a + 1)

            with act.Fori(0, NB - 1) as a:
                project(a)
            split_q(0)
            project(NB - 1)

            act.wait_ge(s_sc, 9)
            std(ln_a, NB + 1)
            norm_x(NB + 1)
            split_kv(NB, 0, 0)
            split_kv(NB, 1, 0)
            split_q(1)
            split_att(0, 0)
            keep_q(NB, 0)
            split_att(0, 1)
            split_x(NB + 1, yp)
            std(ln_o, 0)
            norm(ln_o, 0, ob, ob, s_on)
            std(ln_a, NB + 2)
            std(ln_2, 0)
            norm(ln_2, 0, ob, x1n, s_xn2)
            keep_x1(0)
            split_kv(NB, 2, 0)
            split_x2(0)
            norm_x(NB + 2)
            for n in range(0, 7):
                hidden(0, n)
            split_kv(NB, 3, 0)
            split_att(1, 0)
            hidden(0, 7)
            hidden(0, 8)
            split_q(2)
            act.wait_ge(s_acc, NB * T + 3)
            split_kv(NB + 1, 0, 1)
            hidden(0, 9)
            split_att(1, 1)
            act.wait_ge(s_acc, (NB + 1) * T)
            split_kv(NB + 1, 1, 1)
            keep_q(NB + 1, 1)
            std(ln_a, NB + 3)
            hidden(0, 10)
            split_kv(NB + 1, 2, 1)
            hidden(0, 11)
            split_kv(NB + 1, 3, 1)
            std(ln_o, 1)
            hidden(0, 12)
            norm(ln_o, 1, ob, ob, s_on)
            split_x(NB + 2)
            hidden(0, 13)
            split_att(2, 0)
            std(ln_2, 1)
            hidden(0, 14)
            norm(ln_2, 1, ob, x1n, s_xn2)
            split_q(3)
            act.wait_ge(s_acc, (NB + 1) * T + 3)
            split_kv(NB + 2, 0, 2)
            norm_x(NB + 3)
            hidden(0, 15)
            act.wait_ge(s_acc, (NB + 2) * T)
            split_kv(NB + 2, 1, 2)
            split_kv(NB + 2, 2, 2)
            split_x2(1)
            split_kv(NB + 2, 3, 2)
            split_att(2, 1)
            keep_q(NB + 2, 2)
            hidden(1, 0)
            split_x(NB + 3)
            for n in range(1, 4):
                hidden(1, n)
            std(ln_f, 0, ocs[:, 2:3])
            for n in range(4, 8):
                hidden(1, n)
            norm_y(0)

            def both(f, pos, last):
                c, a = f + 1, f + (NB + 2)
                hidden(f, 8)
                keep_x1(f)
                std(ln_o, c)
                hidden(f, 9)
                norm(ln_o, c, ob, ob, s_on)
                split_kv(a, 0, pos)
                split_kv(a, 1, pos)
                hidden(f, 10)
                split_att(c + 1, 0)
                hidden(f, 11)
                std(ln_2, c)
                norm(ln_2, c, ob, x1n, s_xn2)
                split_kv(a, 2, pos)
                split_att(c + 1, 1)
                hidden(f, 12)
                split_kv(a, 3, pos)
                hidden(f, 13)
                split_x2(c)
                if not last:
                    std(ln_a, a + 1)
                    norm_x(a + 1)
                hidden(f, 14)
                split_q(c + 2)
                keep_q(a, pos)
                hidden(f, 15)
                if not last:
                    split_x(a + 1)
                ff_end(f)

            def ff_at(f, attention, next_q):
                c = f + 1
                hidden(f, 8)
                keep_x1(f)
                std(ln_o, c)
                hidden(f, 9)
                norm(ln_o, c, ob, ob, s_on)
                hidden(f, 10)
                if attention:
                    split_att(c + 1, 0)
                std(ln_2, c)
                hidden(f, 11)
                norm(ln_2, c, ob, x1n, s_xn2)
                hidden(f, 12)
                hidden(f, 13)
                if attention:
                    split_att(c + 1, 1)
                split_x2(c)
                hidden(f, 14)
                if next_q:
                    split_q(c + 2)
                hidden(f, 15)
                ff_end(f)

            with act.Fori(1, NB - 3) as f:
                both(f, f + 2, False)
            both(NB - 3, NB - 1, True)
            with act.Fori(NB - 2, NCH - 3) as f:
                ff_at(f, True, True)
            ff_at(NCH - 3, True, False)
            ff_at(NCH - 2, False, False)
            f = NCH - 1
            hidden(f, KF)
            keep_x1(f)
            for n in range(KF + 1, 2 * KF):
                hidden(f, n)
            std(ln_f, f, ocs[:, 2:3])
            norm_y(f)

        @block.vector
        def _(dve):
            def low(dst, src, hi, sign_op=None, scalar=0.0):
                return nc.vector.scalar_tensor_tensor(out=dst, in0=src, scalar=scalar, in1=hi,
                                                      op0=sign_op, op1=ALU.subtract)

            def moments(ln, tiles, ts=range(T)):
                for t in ts:
                    nc.vector.bn_stats(ln.stats[:, t, :], tiles[t]).then_inc(ln.s_stats, 1)

            def variance(ln, n):
                dve.wait_ge(ln.s_stats, n * T + T)
                even, odd = ln.stats[:, :, 1], ln.stats[:, :, 4]
                nc.vector.tensor_tensor(ln.d[:, 1, :], even, odd, ALU.subtract).then_inc(ln.s_d, 1)
                nc.vector.tensor_tensor(ln.d[:, 2, :], ln.stats[:, :, 2], ln.stats[:, :, 5], ALU.add
                                        ).then_inc(ln.s_d, 1)
                nc.vector.tensor_tensor(ln.d[:, 0, :], even, odd, ALU.add).then_inc(ln.s_d, 1)
                dve.wait_ge(ln.s_d, n * 3 + 3)
                nc.vector.tensor_tensor(ln.d[:, 3, :], ln.d[:, 1, :], ln.d[:, 1, :], ALU.mult).then_inc(ln.s_d2, 1)
                dve.wait_ge(ln.s_d2, n + 1)
                nc.vector.scalar_tensor_tensor(out=ln.var[:], in0=ln.d[:, 3, :], scalar=E / 4.0, in1=ln.d[:, 2, :],
                                               op0=ALU.mult, op1=ALU.add).then_inc(ln.s_var, 1)

            def stats(ln, n, tiles):
                moments(ln, tiles)
                variance(ln, n)

            def rstd(ln, n):
                dve.wait_ge(ln.s_std, n + 1)
                nc.vector.reciprocal(ln.rstd[:], ln.std[:]).then_inc(ln.s_rstd, 1)
                dve.wait_ge(ln.s_rstd, n + 1)

            def shift(ln, n, by):
                nc.vector.scalar_tensor_tensor(out=ln.nmr[:], in0=ln.d[:, 0, :], scalar=-0.5, in1=by,
                                               op0=ALU.mult, op1=ALU.mult).then_inc(ln.s_nmr, 1)

            def scale_shift(ln, n):
                rstd(ln, n)
                shift(ln, n, ln.rstd[:])

            def norm_x_stats(a):
                dve.wait_ge(s_xa, a * 16 + 16)
                stats(ln_a, a, [xa[:, t, :] for t in range(T)])

            def split_x(a, banks=wp):
                for h in range(KE):
                    dve.wait_ge(s_xth, a * KE + h + 1)
                    nc.vector.tensor_tensor(xt_lo[:, h, :], banks[h][:], xt_hi[:, h, :].bitcast(F32), ALU.subtract
                                            ).then_inc(s_xtl, 1)

            def bias_kv(a, t, banks):
                b = t % 2
                if t >= 2:
                    dve.wait_ge(s_lo, (a * T + t - 1) * 3)
                dve.wait_ge(s_kvp, a * T + t + 1)
                nc.vector.tensor_tensor(kv[:, b, :], banks[t % len(banks)][:], bkv_row[:], ALU.add).then_inc(s_kv, 1)

            def split_kv(a, t, pos):
                b = t % 2
                dve.wait_ge(s_hi, (a * T + t + 1) * 3)
                low(k_lo[:, b, :], kv[:, b, 0:E], k_hi[:, b, :].bitcast(F32), ALU.max).then_inc(s_lo, 1)
                v = kv[:, b, E:2 * E].rearrange("p (h c) -> p h c", h=KE)
                for s in range(2):
                    at = pos_cols[:, bass.ds(pos, 1), t, s:s + 1].rearrange("p o s -> p (o s)")
                    low(v_lo[:, b, :, s, 0:P], v, v_hi[:, b, :, s, 0:P].bitcast(F32), ALU.mult, at
                        ).then_inc(s_lo, 1)

            def head_matrices(b):
                dve.wait_ge(s_accz, b + 1)
                after(dve, s_atp, b * NB * G)
                after(dve, s_atl, b * NB * KE)
                for h in range(KE):
                    nc.vector.tensor_copy(kv_sum[:, h].rearrange("p s c -> p (s c)"), acc[h][:, 0:2 * VW]
                                          ).then_inc(s_sum, 1)
                dve.wait_ge(s_sum, (b + 1) * KE)
                for g in range(G):
                    r0, h = (g % 2) * GW, g // 2
                    src = slice(r0, r0 + GW)
                    num = slice(r0, r0 + GW)
                    dn = slice(GW - r0, 2 * GW - r0)
                    for s in range(2):
                        o0 = r0 if s == 0 else GW - r0
                        dst = slice(o0, o0 + GW)
                        nc.vector.tensor_tensor(kvt[dst, g, num], kv_sum[src, h, s, r0:r0 + GW], mask[src, :],
                                                ALU.mult).then_inc(s_kvt, 1)
                        nc.vector.tensor_scalar(kvt[dst, g, dn], mask[src, :], kv_sum[src, h, s, P:P + 1], None,
                                                ALU.mult).then_inc(s_kvt, 1)
                dve.wait_ge(s_kvt, (b + 1) * 4 * G)
                nc.vector.tensor_copy(kvt_hi[:], kvt[:]).then_inc(s_kvh, 1)
                dve.wait_ge(s_kvh, b + 1)
                nc.vector.tensor_tensor(kvt_lo[:], kvt[:], kvt_hi[:].bitcast(F32), ALU.subtract).then_inc(s_kvl, 1)

            def q_cos(c, pos, groups=range(G)):
                dve.wait_ge(s_rows, c * 16 + 16)
                after(dve, s_ql, c * G)
                for g in groups:
                    r0 = (g % 2) * GW
                    nc.vector.tensor_tensor(qsc[GW - r0:2 * GW - r0, g, :],
                                            q_all[r0:r0 + GW, g // 2, bass.ds(pos * CH, CH)],
                                            pos_rows[r0:r0 + GW, 1, :], ALU.mult).then_inc(s_qc, 1)

            def denominators(c, k):
                for g in (2 * k, 2 * k + 1):
                    r0 = (g % 2) * GW
                    dve.wait_ge(s_atp, c * G + g + 1)
                    nc.vector.tensor_scalar(att[r0:r0 + GW, k, :], yp[g % 2][GW - r0:2 * GW - r0, :], EPS_DEN, None,
                                            ALU.max).then_inc(s_den, 1)

            def invert(c, k):
                dve.wait_ge(s_den, c * G + 2 * k + 2)
                nc.vector.reciprocal(att[:, k, :], att[:, k, :]).then_inc(s_rden, 1)

            def quotients(c, k):
                dve.wait_ge(s_rden, c * KE + k + 1)
                for g in (2 * k, 2 * k + 1):
                    r0 = (g % 2) * GW
                    nc.vector.tensor_tensor(att[r0:r0 + GW, k, :], yp[g % 2][r0:r0 + GW, :], att[r0:r0 + GW, k, :],
                                            ALU.mult).then_inc(s_att, 1)

            def divide(c, k, between=lambda: None):
                denominators(c, k)
                invert(c, k)
                between()
                quotients(c, k)

            def split_att(c, k):
                dve.wait_ge(s_ath, c * KE + k + 1)
                nc.vector.tensor_tensor(att_lo[:, k, :], att[:, k, :], att_hi[:, k, :].bitcast(F32),
                                        ALU.subtract).then_inc(s_atl, 1)

            def bias_o(c):
                after(dve, s_x2p, c * KE)
                for i in range(2):
                    dve.wait_ge(s_op, c * 2 + i + 1)
                    nc.vector.tensor_tensor(
                        ob[:, 2 * i:2 * i + 2, :], wp[i][:].rearrange("p (t e) -> p t e", t=2),
                        bo_row[:].rearrange("p (o e) -> p o e", o=1).to_broadcast([P, 2, E]), ALU.add
                    ).then_inc(s_ob, 1)
                    dve.wait_ge(s_ob, c * 2 + i + 1)
                    moments(ln_o, [ob[:, t, :] for t in range(T)], (2 * i, 2 * i + 1))
                variance(ln_o, c)

            def stats_x1(c):
                for t in range(T):
                    dve.wait_ge(s_x1n, c * T + t + 1)
                    moments(ln_2, [x1n[:, t, :] for t in range(T)], (t,))
                variance(ln_2, c)

            def split_x2(c):
                for h in range(KE):
                    dve.wait_ge(s_x2h, c * KE + h + 1)
                    nc.vector.tensor_tensor(x2_lo[:, h, :], wp[h][:], x2_hi[:, h, :], ALU.subtract
                                            ).then_inc(s_x2l, 1)

            def hidden(f, n):
                dve.wait_ge(s_hh, f * 2 * KF + n + 1)
                hi, lo = (h1_hi, h1_lo) if n < KF else (h2_hi, h2_lo)
                low(lo[:, n % KF, :], hidden_bank(n)[:], hi[:, n % KF, :], ALU.max).then_inc(s_hl, 1)

            y_tiles = [yp[t // 2][:, (t % 2) * E:(t % 2 + 1) * E] for t in range(T)]

            def moments_y(f, i):
                dve.wait_ge(s_yp, f * T + 2 * i + 2)
                moments(ln_f, y_tiles, (2 * i, 2 * i + 1))

            def scale_shift_y(f):
                rstd(ln_f, f)
                nc.vector.tensor_scalar(ln_f.std[:], ln_f.rstd[:], ocs[:, 1:2], None, ALU.mult).then_inc(s_fc, 1)
                dve.wait_ge(s_fc, f + 1)
                shift(ln_f, f, ln_f.std[:])

            def split_w(n):
                lo, full, hi = ((wkv_lo, wkv_f, wkv_hi), (wq_lo, wq_f, wq_hi), (wo_lo, wo_f, wo_hi))[n]
                dve.wait_ge(s_whi, n + 1)
                nc.vector.tensor_tensor(lo[:], full, hi[:].bitcast(F32), ALU.subtract).then_inc(s_wlo, 1)

            nc.vector.memset(zero_l[:].bitcast(U32), 0).then_inc(s_zero, 1)
            nc.vector.memset(eps_col[:], EPS_LN).then_inc(s_zero, 1)
            norm_x_stats(0)
            scale_shift(ln_a, 0)
            split_w(0)
            split_x(0)
            dve.wait_ge(s_first, 16 * FIRST_LOADS)
            split_w(1)
            nc.vector.tensor_copy(pos_hi[:], pos_cols[:]).then_inc(s_poshi, 1)
            dve.wait_ge(s_poshi, 1)
            nc.vector.tensor_tensor(pos_lo[:], pos_cols[:], pos_hi[:].bitcast(F32), ALU.subtract).then_inc(s_poslo, 1)
            split_w(2)

            def project(a, between=lambda: None):
                norm_x_stats(a + 1)
                bias_kv(a, 0, wide)
                bias_kv(a, 1, wide)
                split_kv(a, 0, a)
                scale_shift(ln_a, a + 1)
                split_kv(a, 1, a)
                bias_kv(a, 2, wide)
                between()
                bias_kv(a, 3, wide)
                split_kv(a, 2, a)
                split_kv(a, 3, a)
                split_x(a + 1)

            with dve.Fori(0, NB - 3) as a:
                project(a)
            project(NB - 3, lambda: q_cos(0, 0, (0, 1)))
            project(NB - 2, lambda: q_cos(0, 0, (2, 3)))
            project(NB - 1, lambda: q_cos(1, 1, (0, 1)))

            dve.wait_ge(s_sc, 9)
            head_matrices(0)
            norm_x_stats(NB + 1)
            bias_kv(NB, 0, ffp)
            scale_shift(ln_a, NB + 1)
            denominators(0, 0)
            invert(0, 0)
            quotients(0, 0)
            split_kv(NB, 0, 0)
            q_cos(1, 1, (2, 3))
            bias_kv(NB, 1, ffp)
            denominators(0, 1)
            invert(0, 1)
            quotients(0, 1)
            split_att(0, 0)
            split_att(0, 1)
            bias_kv(NB, 2, ffp)
            split_kv(NB, 1, 0)
            split_x(NB + 1, yp)
            bias_o(0)
            scale_shift(ln_o, 0)
            denominators(1, 0)
            bias_kv(NB, 3, ffp)
            norm_x_stats(NB + 2)
            stats_x1(0)
            scale_shift(ln_2, 0)
            invert(1, 0)
            scale_shift(ln_a, NB + 2)
            quotients(1, 0)
            split_x2(0)
            q_cos(2, 2)
            for n in range(0, 4):
                hidden(0, n)
            split_kv(NB, 2, 0)
            hidden(0, 4)
            hidden(0, 5)
            denominators(1, 1)
            hidden(0, 6)
            split_kv(NB, 3, 0)
            hidden(0, 7)
            hidden(0, 8)
            invert(1, 1)
            dve.wait_ge(s_lo, (NB * T + 3) * 3)
            bias_kv(NB + 1, 0, wp)
            dve.wait_ge(s_lo, ((NB + 1) * T) * 3)
            bias_kv(NB + 1, 1, wp)
            quotients(1, 1)
            split_kv(NB + 1, 0, 1)
            split_kv(NB + 1, 1, 1)
            split_att(1, 0)
            bias_kv(NB + 1, 2, wp)
            bias_kv(NB + 1, 3, wp)
            norm_x_stats(NB + 3)
            split_att(1, 1)
            hidden(0, 9)
            q_cos(3, 3)
            split_kv(NB + 1, 2, 1)
            scale_shift(ln_a, NB + 3)
            hidden(0, 10)
            hidden(0, 11)
            bias_o(1)
            denominators(2, 0)
            scale_shift(ln_o, 1)
            invert(2, 0)
            hidden(0, 12)
            quotients(2, 0)
            stats_x1(1)
            split_x(NB + 2)
            scale_shift(ln_2, 1)
            hidden(0, 13)
            split_kv(NB + 1, 3, 1)
            hidden(0, 14)
            dve.wait_ge(s_lo, ((NB + 1) * T + 3) * 3)
            bias_kv(NB + 2, 0, wp)
            denominators(2, 1)
            dve.wait_ge(s_lo, ((NB + 2) * T) * 3)
            bias_kv(NB + 2, 1, wp)
            invert(2, 1)
            split_kv(NB + 2, 0, 2)
            bias_kv(NB + 2, 2, wp)
            quotients(2, 1)
            split_kv(NB + 2, 1, 2)
            bias_kv(NB + 2, 3, wp)
            hidden(0, 15)
            split_kv(NB + 2, 2, 2)
            split_x2(1)
            moments_y(0, 0)
            split_att(2, 0)
            split_kv(NB + 2, 3, 2)
            split_att(2, 1)
            hidden(1, 0)
            split_x(NB + 3)
            moments_y(0, 1)
            variance(ln_f, 0)
            for n in range(1, 4):
                hidden(1, n)
            scale_shift_y(0)
            for n in range(4, 8):
                hidden(1, n)

            def ff_end(f):
                hidden(f + 1, 0)
                moments_y(f, 1)
                variance(ln_f, f)
                for n in range(1, KF):
                    hidden(f + 1, n)
                    if n == 5:
                        scale_shift_y(f)

            def both(f, pos, pos_q, last):
                c, a = f + 1, f + (NB + 2)
                hidden(f, 8)
                bias_o(c)
                scale_shift(ln_o, c)
                hidden(f, 9)
                divide(c + 1, 0, lambda: (bias_kv(a, 0, wp), bias_kv(a, 1, wp)))
                split_kv(a, 0, pos)
                hidden(f, 10)
                split_kv(a, 1, pos)
                stats_x1(c)
                split_att(c + 1, 0)
                hidden(f, 11)
                scale_shift(ln_2, c)
                divide(c + 1, 1, lambda: bias_kv(a, 2, wp))
                split_kv(a, 2, pos)
                bias_kv(a, 3, wp)
                hidden(f, 12)
                split_att(c + 1, 1)
                split_kv(a, 3, pos)
                hidden(f, 13)
                split_x2(c)
                if not last:
                    norm_x_stats(a + 1)
                    scale_shift(ln_a, a + 1)
                q_cos(c + 2, pos_q)
                hidden(f, 14)
                hidden(f, 15)
                if last:
                    head_matrices(1)
                moments_y(f, 0)
                if not last:
                    split_x(a + 1)
                ff_end(f)

            def ff_at(f, attention, pos_q):
                c = f + 1
                hidden(f, 8)
                bias_o(c)
                scale_shift(ln_o, c)
                hidden(f, 9)
                if attention:
                    divide(c + 1, 0)
                hidden(f, 10)
                stats_x1(c)
                if attention:
                    split_att(c + 1, 0)
                hidden(f, 11)
                scale_shift(ln_2, c)
                if attention:
                    divide(c + 1, 1, lambda: hidden(f, 12))
                else:
                    hidden(f, 12)
                hidden(f, 13)
                if attention:
                    split_att(c + 1, 1)
                if pos_q is not None:
                    q_cos(c + 2, pos_q)
                split_x2(c)
                hidden(f, 14)
                hidden(f, 15)
                moments_y(f, 0)
                ff_end(f)

            with dve.Fori(1, NB - 3) as f:
                both(f, f + 2, f + 3, False)
            both(NB - 3, NB - 1, 0, True)
            with dve.Fori(NB - 2, NCH - 3) as f:
                ff_at(f, True, f - (NB - 3))
            ff_at(NCH - 3, True, None)
            ff_at(NCH - 2, False, None)
            f = NCH - 1
            for n in range(KF, 2 * KF):
                hidden(f, n)
            moments_y(f, 0)
            moments_y(f, 1)
            variance(ln_f, f)
            scale_shift_y(f)

        @block.gpsimd
        def _(pool):
            def pos_in_v(a, pos, ts=range(T)):
                for t in ts:
                    b = t % 2
                    after(pool, s_acc, a * T + t - 1)
                    here = (slice(None), bass.ds(pos, 1), t, slice(None))
                    whole = pos_cols[here].to_broadcast([P, KE, 2])
                    for v, other in ((v_hi, pos_lo), (v_lo, pos_hi)):
                        part = other[:].bitcast(F32)[here].to_broadcast([P, KE, 2])
                        nc.gpsimd.tensor_tensor(v[:, b, :, :, P], whole, part, ALU.subtract).then_inc(s_pc, 1)

            def q_sin(c, pos, steps):
                if steps is not None:
                    pool.wait_ge(s_pc, steps * 2)
                pool.wait_ge(s_rows, c * 16 + 16)
                pool.wait_ge(s_q, c * KE + KE)
                after(pool, s_ql, c * G)
                for g in range(G):
                    r0 = (g % 2) * GW
                    nc.gpsimd.tensor_tensor(qsc[r0:r0 + GW, g, :], q_all[r0:r0 + GW, g // 2, bass.ds(pos * CH, CH)],
                                            pos_rows[r0:r0 + GW, 0, :], ALU.mult).then_inc(s_qs, 1)
                    pool.wait_ge(s_qs, c * G + g + 1)

            def split_q(c):
                for g in range(G):
                    pool.wait_ge(s_qh, c * G + g + 1)
                    nc.gpsimd.tensor_tensor(qsc_lo[:, g, :], qsc[:, g, :], qsc_hi[:, g, :].bitcast(F32),
                                            ALU.subtract).then_inc(s_ql, 1)

            def add_x(c):
                pool.wait_ge(s_xr, c * 16 + 16)
                for t in range(T):
                    pool.wait_ge(s_on, c * T + t + 1)
                    nc.gpsimd.tensor_tensor(x1n[:, t, :], ob[:, t, :], x1n[:, t, :], ALU.add).then_inc(s_x1n, 1)

            def add_x1(f):
                pool.wait_ge(s_fo, f * T + 2 * T)
                pool.wait_ge(s_x1, f + 1)
                nc.gpsimd.tensor_tensor(fo[:], fo[:], x1[:], ALU.add).then_inc(s_out, 1)
                pool.wait_ge(s_out, f + 2)

            def w0_halves():
                nc.gpsimd.tensor_scalar(w0_half, k0_u8, sgn[:, 0:1], 0.0, ALU.mult, ALU.add).then_inc(s_w0h, 1)

            def w0_difference():
                pool.wait_ge(s_w0h, 1)
                nc.gpsimd.tensor_tensor(w0[:], w0_half[:, 0:KE], w0_half[:, KE:2 * KE], ALU.subtract).then_inc(s_ffw, 1)

            def w1_part(n):
                m = slice(n * KF // 2, (n + 1) * KF // 2)
                nc.gpsimd.tensor_scalar(w1[:, m], k1_u8[:, m], ksc[:, 0:1], ksc[:, 1:2], ALU.mult, ALU.add
                                        ).then_inc(s_ffw, 1)

            def w2_whole():
                nc.gpsimd.tensor_scalar(w2[:], k2_u8, 2.0, -1.0, ALU.mult, ALU.add).then_inc(s_ffw, 1)

            def scale_terms():
                pool.wait_ge(s_scales, 16 * SCALE_LOADS)
                nc.gpsimd.tensor_scalar(sgn[:], sv[:], 0.0, 2.0, ALU.is_ge, ALU.mult).then_inc(s_sc, 1)
                pool.wait_ge(s_sc, 1)
                nc.gpsimd.tensor_scalar(sgn[:], sgn[:], -1.0, None, ALU.add).then_inc(s_sc, 1)
                pool.wait_ge(s_sc, 2)
                nc.gpsimd.tensor_tensor(sab[:], sv[:], sgn[:], ALU.mult).then_inc(s_sc, 1)
                nc.gpsimd.tensor_scalar(ksc[:, 0:1], sgn[:, 1:2], 2.0 * H1_SCALE, None, ALU.mult).then_inc(s_sc, 1)
                nc.gpsimd.tensor_scalar(ksc[:, 1:2], sgn[:, 1:2], -H1_SCALE, None, ALU.mult).then_inc(s_sc, 1)
                pool.wait_ge(s_sc, 5)
                nc.gpsimd.tensor_tensor(ocs[:, 0:1], sab[:, 0:1], sab[:, 1:2], ALU.mult).then_inc(s_sc, 1)
                pool.wait_ge(s_sc, 6)
                nc.gpsimd.tensor_scalar(ocs[:, 1:2], ocs[:, 0:1], sv[:, 2:3], OUT_SCALE, ALU.mult, ALU.mult
                                        ).then_inc(s_sc, 1)
                pool.wait_ge(s_sc, 7)
                nc.gpsimd.tensor_tensor(ocs[:, 2:3], ocs[:, 1:2], ocs[:, 1:2], ALU.mult).then_inc(s_sc, 1)
                pool.wait_ge(s_sc, 8)
                nc.gpsimd.tensor_scalar(ocs[:, 2:3], ocs[:, 2:3], 1.0 / E, None, ALU.mult).then_inc(s_sc, 1)

            scale_terms()
            pool.wait_ge(s_poslo, 1)
            pool.sem_inc(s_out, 1)
            pos_in_v(0, 0)
            pool.wait_ge(s_sc, 5)
            pool.wait_ge(s_late, 16 * LATE_LOADS)
            parts = (w0_halves, w0_difference, lambda: w1_part(0), lambda: w1_part(1), w2_whole)
            for a, part in enumerate(parts, 1):
                pos_in_v(a, a, (0, 1))
                part()
                pos_in_v(a, a, (2, 3))
            a = len(parts) + 1
            pos_in_v(a, a, (0, 1))
            pool.wait_ge(s_wlo, 3)
            q_sin(0, 0, a * T + 2)
            pos_in_v(a, a, (2, 3))
            split_q(0)
            pos_in_v(NB - 1, NB - 1)

            pos_in_v(NB, 0, (0,))
            q_sin(1, 1, NB * T + 1)
            split_q(1)
            pos_in_v(NB, 0, (1,))
            q_sin(2, 2, NB * T + 2)
            add_x(0)
            pos_in_v(NB, 0, (2, 3))
            pos_in_v(NB + 1, 1, (0,))
            split_q(2)
            pos_in_v(NB + 1, 1, (1, 2))
            add_x(1)
            pos_in_v(NB + 1, 1, (3,))
            q_sin(3, 3, (NB + 2) * T)
            split_q(3)
            pos_in_v(NB + 2, 2, (0, 1, 2, 3))
            add_x1(0)

            def both(f, pos_q):
                c, a = f + 1, f + (NB + 2)
                pos_in_v(a, c + 1, (0, 1))
                add_x(c)
                pool.wait_ge(s_x1n, c * T + T)
                q_sin(c + 2, pos_q, None)
                pos_in_v(a, c + 1, (2, 3))
                split_q(c + 2)
                add_x1(f)

            with pool.Fori(1, NB - 3) as f:
                both(f, f + 3)
            both(NB - 3, 0)
            with pool.Fori(NB - 2, NCH - 3) as f:
                add_x(f + 1)
                pool.wait_ge(s_x1n, f * T + 2 * T)
                q_sin(f + 3, f - (NB - 3), None)
                split_q(f + 3)
                add_x1(f)
            for f in (NCH - 3, NCH - 2):
                add_x(f + 1)
                add_x1(f)
            add_x1(NCH - 1)


def kernel(L0_attn_x, L0_attn_Wq, L0_attn_bq, L0_attn_Wk, L0_attn_bk, L0_attn_Wv, L0_attn_bv, L0_attn_Wo,
           L0_attn_bo, L0_ffn_k0, L0_ffn_k1, L0_ffn_k2, L0_ffn_s0, L0_ffn_s1, L0_ffn_s2):
    import concourse.bacc as bacc
    from concourse.bass_utils import run_bass_kernel_spmd

    def a(v):
        return np.asarray(v)

    def rows(*v):
        return np.ascontiguousarray(np.concatenate([a(u).reshape(1, -1) for u in v], axis=1))

    pos_rows, pos_cols, ident, mask = shape_tables()
    arrays = {
        "x": np.ascontiguousarray(a(L0_attn_x).reshape(B * L, E)),
        "wq_t": np.ascontiguousarray(a(L0_attn_Wq).T),
        "wkv_t": np.ascontiguousarray(np.concatenate([a(L0_attn_Wk).T, a(L0_attn_Wv).T], axis=1)),
        "wo_t": np.ascontiguousarray(a(L0_attn_Wo).T),
        "bq": a(L0_attn_bq),
        "bkv": rows(L0_attn_bk, L0_attn_bv),
        "bo": rows(L0_attn_bo),
        "k0": np.ascontiguousarray(a(L0_ffn_k0)).view(np.uint32),
        "k1": np.ascontiguousarray(a(L0_ffn_k1)).view(np.uint32),
        "k2": np.ascontiguousarray(a(L0_ffn_k2)).view(np.uint32),
        "s0": a(L0_ffn_s0).reshape(1, 1),
        "s1": a(L0_ffn_s1).reshape(1, 1),
        "s2": a(L0_ffn_s2).reshape(1, 1),
        "pos_rows_in": pos_rows, "pos_cols_in": pos_cols, "ident_in": ident, "mask_in": mask,
    }
    nc = bacc.Bacc("TRN2", target_bir_lowering=False, num_devices=1)
    d = {n: nc.dram_tensor(n, list(v.shape), mybir.dt.from_np(v.dtype), kind="ExternalInput").ap()
         for n, v in arrays.items()}
    out = nc.dram_tensor("out", [B * L, E], F32, kind="ExternalOutput").ap()
    build(nc, d["x"], d["wq_t"], d["wkv_t"], d["wo_t"], d["bq"], d["bkv"], d["bo"], d["k0"], d["k1"], d["k2"],
          (d["s0"], d["s1"], d["s2"]), d["pos_rows_in"], d["pos_cols_in"], d["ident_in"], d["mask_in"], out)
    r = run_bass_kernel_spmd(nc, [arrays], core_ids=[0])
    return r.results[0]["out"].reshape(B, L, E)
```
